# Optimizing a Trainium2 kernel written in Bass

```python
import numpy as np
import jax
import jax.numpy as jnp

def _softmax(x, axis=-1):
    return jax.nn.softmax(x, axis=axis)

def _gelu(x):
    return jax.nn.gelu(x, approximate=True)

def _silu(x):
    return jax.nn.silu(x)

def _sigmoid(x):
    return jax.nn.sigmoid(x)

def _layernorm(x, axis=-1, eps=1e-05):
    m = jnp.mean(x, axis=axis, keepdims=True)
    v = jnp.var(x, axis=axis, keepdims=True)
    return (x - m) / jnp.sqrt(v + eps)

def _scatter_add(tgt, idx, src, axis=0):
    return tgt.at[idx].add(src)

def _segment_sum(src, seg, n):
    return jax.ops.segment_sum(src, seg, n)
kernel_name = 'mk_audio_tower_d1_tok_aud1d512_r4_1fe26c'

def setup_inputs(seed: int=0):
    np.random.seed(seed)
    _w = jnp.asarray

    def _rec_inputs():
        import jax
        import jax.numpy as jnp
        _rk = jax.random.key(seed)
        x = -0.00238186 + 1.00146 * jax.random.normal(jax.random.fold_in(_rk, 1), (64, 5000), jnp.float32)
        return x
    x = _rec_inputs()

    def _L0_tok_setup():
        import jax, jax.numpy as jnp
        import numpy as np
        B, E, G, P = (8, 16, 5000, 128)
        MASK_DENSITY = 0.1
        key = jax.random.key(seed)
        k_x, k_w, k_m = jax.random.split(key, 3)
        x = jax.random.normal(k_x, (B, G), dtype=jnp.float32)
        weight = jax.random.normal(k_w, (E, G, P), dtype=jnp.float32) * 0.01
        bias = jnp.zeros((E, P), dtype=jnp.float32)
        mask = (jax.random.uniform(k_m, (G, P)) < MASK_DENSITY).astype(jnp.float32)
        return {'x': x, 'weight': weight, 'bias': bias, 'mask': mask}
    _L0_tok_all = _L0_tok_setup()
    _L0_tok_in = {k: v for k, v in _L0_tok_all.items() if k in ('weight', 'bias', 'mask')}
    del _L0_tok_all

    def _L0_attn_setup():
        import jax, jax.numpy as jnp
        import numpy as np
        DIM = 128
        HEADS = 8
        DIM_HEAD = 64
        DIM_INNER = HEADS * DIM_HEAD
        FRAC_GRAD = 0.5
        SCALE = DIM_HEAD ** (-0.5)
        EPS_CUMPROD = 1e-10
        EPS_INV = 1e-08

        def _rms_norm(x, gamma):
            nrm = jnp.linalg.norm(x, axis=-1, keepdims=True)
            return x / jnp.maximum(nrm, 1e-12) * DIM ** 0.5 * gamma

        def _safe_cumprod(t, axis):
            t = jnp.clip(t, EPS_CUMPROD, 1.0)
            return jnp.exp(jnp.cumsum(jnp.log(t), axis=axis))
        key = jax.random.key(seed)
        ks = jax.random.split(key, 8)
        b, n = (2, 512)
        x = jax.random.normal(ks[0], (b, n, DIM), dtype=jnp.float32)
        gamma = jnp.ones((DIM,), dtype=jnp.float32)
        w_qkv = jax.random.normal(ks[1], (DIM, 3 * DIM_INNER), dtype=jnp.float32) * 0.02
        b_qkv = jnp.zeros((3 * DIM_INNER,), dtype=jnp.float32)
        w_a = jax.random.normal(ks[2], (DIM, DIM_INNER), dtype=jnp.float32) * 0.02
        b_a = jnp.full((DIM_INNER,), 2.0, dtype=jnp.float32)
        w_out = jax.random.normal(ks[3], (DIM_INNER, DIM), dtype=jnp.float32) * 0.02
        b_out = jnp.zeros((DIM,), dtype=jnp.float32)
        return {'x': x, 'gamma': gamma, 'w_qkv': w_qkv, 'b_qkv': b_qkv, 'w_a': w_a, 'b_a': b_a, 'w_out': w_out, 'b_out': b_out}
    _L0_attn_all = _L0_attn_setup()
    _L0_attn_in = {k: v for k, v in _L0_attn_all.items() if k in ('gamma', 'w_qkv', 'b_qkv', 'w_a', 'b_a', 'w_out', 'b_out')}
    del _L0_attn_all

    def _L0_ffn_setup():
        import jax, jax.numpy as jnp
        import numpy as np
        B, S, D, F, E = (4, 512, 128, 512, 8)
        key = jax.random.key(seed)
        k = jax.random.split(key, 5)
        x = jax.random.normal(k[0], (B, S, D), dtype=jnp.float32)
        Ws = jax.random.normal(k[1], (D, E), dtype=jnp.float32) * 0.02
        bs = jnp.zeros((E,), dtype=jnp.float32)
        W1 = jax.random.normal(k[2], (E, D, F), dtype=jnp.float32) * 0.02
        b1 = jnp.zeros((E, F), dtype=jnp.float32)
        W2 = jax.random.normal(k[3], (E, F, D), dtype=jnp.float32) * 0.02
        b2 = jnp.zeros((E, D), dtype=jnp.float32)
        return {'x': x, 'Ws': Ws, 'bs': bs, 'W1': W1, 'b1': b1, 'W2': W2, 'b2': b2}
    _L0_ffn_all = _L0_ffn_setup()
    _L0_ffn_in = {k: v for k, v in _L0_ffn_all.items() if k in ('Ws', 'bs', 'W1', 'b1', 'W2', 'b2')}
    del _L0_ffn_all
    return {'x': x, 'L0_tok_weight': _L0_tok_in['weight'], 'L0_tok_bias': _L0_tok_in['bias'], 'L0_tok_mask': _L0_tok_in['mask'], 'L0_attn_gamma': _L0_attn_in['gamma'], 'L0_attn_w_qkv': _L0_attn_in['w_qkv'], 'L0_attn_b_qkv': _L0_attn_in['b_qkv'], 'L0_attn_w_a': _L0_attn_in['w_a'], 'L0_attn_b_a': _L0_attn_in['b_a'], 'L0_attn_w_out': _L0_attn_in['w_out'], 'L0_attn_b_out': _L0_attn_in['b_out'], 'L0_ffn_Ws': _L0_ffn_in['Ws'], 'L0_ffn_bs': _L0_ffn_in['bs'], 'L0_ffn_W1': _L0_ffn_in['W1'], 'L0_ffn_b1': _L0_ffn_in['b1'], 'L0_ffn_W2': _L0_ffn_in['W2'], 'L0_ffn_b2': _L0_ffn_in['b2']}

def reference(x, L0_tok_weight, L0_tok_bias, L0_tok_mask, L0_attn_gamma, L0_attn_w_qkv, L0_attn_b_qkv, L0_attn_w_a, L0_attn_b_a, L0_attn_w_out, L0_attn_b_out, L0_ffn_Ws, L0_ffn_bs, L0_ffn_W1, L0_ffn_b1, L0_ffn_W2, L0_ffn_b2):
    import jax
    import jax.numpy as jnp

    def _L0_tok_ref(x, weight, bias, mask):
        import jax, jax.numpy as jnp
        import numpy as np
        B, E, G, P = (8, 16, 5000, 128)
        MASK_DENSITY = 0.1
        W = weight * mask[None, :, :]
        out = jnp.einsum('bg,egp->bep', x, W)
        return out + bias[None, :, :]

    def _L0_attn_ref(x, gamma, w_qkv, b_qkv, w_a, b_a, w_out, b_out):
        import jax, jax.numpy as jnp
        import numpy as np
        DIM = 128
        HEADS = 8
        DIM_HEAD = 64
        DIM_INNER = HEADS * DIM_HEAD
        FRAC_GRAD = 0.5
        SCALE = DIM_HEAD ** (-0.5)
        EPS_CUMPROD = 1e-10
        EPS_INV = 1e-08

        def _rms_norm(x, gamma):
            nrm = jnp.linalg.norm(x, axis=-1, keepdims=True)
            return x / jnp.maximum(nrm, 1e-12) * DIM ** 0.5 * gamma

        def _safe_cumprod(t, axis):
            t = jnp.clip(t, EPS_CUMPROD, 1.0)
            return jnp.exp(jnp.cumsum(jnp.log(t), axis=axis))
        b, n, _ = x.shape
        x = _rms_norm(x, gamma)
        qkv = x @ w_qkv + b_qkv
        qkv = qkv.reshape(b, n, 3, HEADS, DIM_HEAD).transpose(2, 0, 3, 1, 4)
        q, k, v = (qkv[0], qkv[1], qkv[2])
        q = q * SCALE
        a = (x @ w_a + b_a).reshape(b, n, HEADS, DIM_HEAD).transpose(0, 2, 1, 3)
        a = a * FRAC_GRAD + jax.lax.stop_gradient(a) * (1.0 - FRAC_GRAD)
        a = jax.nn.sigmoid(a)
        a_cum = _safe_cumprod(a, axis=-2)
        a_cum_inv = 1.0 / jnp.maximum(a_cum, EPS_INV)
        q = q * a_cum
        k = k * a_cum_inv
        sim = jnp.einsum('bhid,bhjd->bhij', q, k)
        causal_mask = jnp.triu(jnp.ones((n, n), dtype=bool), k=1)
        attn = jnp.where(causal_mask, 0.0, sim)
        out = jnp.einsum('bhij,bhjd->bhid', attn, v)
        out = out.transpose(0, 2, 1, 3).reshape(b, n, DIM_INNER)
        return out @ w_out + b_out

    def _L0_ffn_ref(x, Ws, bs, W1, b1, W2, b2):
        import jax, jax.numpy as jnp
        import numpy as np
        B, S, D, F, E = (4, 512, 128, 512, 8)
        Bb, Ss, Dd = x.shape
        xt = x.reshape(-1, Dd)
        logits = xt @ Ws + bs
        probs = jax.nn.softmax(logits, axis=-1)
        prob_max = jnp.max(probs, axis=-1)
        routes = jnp.argmax(probs, axis=-1)
        onehot = jax.nn.one_hot(routes, W1.shape[0], dtype=xt.dtype)

        def expert_ffn(w1, bb1, w2, bb2):
            h = jax.nn.gelu(xt @ w1 + bb1, approximate=False)
            return h @ w2 + bb2
        y = jax.vmap(expert_ffn)(W1, b1, W2, b2)
        out = jnp.einsum('te,etd->td', onehot, y)
        out = out * prob_max[:, None]
        return out.reshape(Bb, Ss, Dd)
    h = _L0_tok_ref(x, L0_tok_weight, L0_tok_bias, L0_tok_mask)
    h = h + _L0_attn_ref(_layernorm(h, axis=-1), L0_attn_gamma, L0_attn_w_qkv, L0_attn_b_qkv, L0_attn_w_a, L0_attn_b_a, L0_attn_w_out, L0_attn_b_out)
    h = h + _L0_ffn_ref(_layernorm(h, axis=-1), L0_ffn_Ws, L0_ffn_bs, L0_ffn_W1, L0_ffn_b1, L0_ffn_W2, L0_ffn_b2)
    return h

_drawn_inputs = setup_inputs


def setup_inputs(seed=0):
    import zlib

    import numpy as np

    out = dict(_drawn_inputs(seed))
    spreads = {'L0_tok_bias': (0.0, 0.1),
     'L0_attn_gamma': (1.0, 0.6),
     'L0_attn_b_qkv': (0.0, 0.1),
     'L0_attn_b_a': (2.0, 0.6),
     'L0_attn_b_out': (0.0, 0.1),
     'L0_ffn_bs': (0.0, 0.1),
     'L0_ffn_b1': (0.0, 0.51),
     'L0_ffn_b2': (0.0, 0.1)}
    factors = {'L0_attn_w_a': 8.0}
    for name, (base, spread) in spreads.items():
        noise = np.random.default_rng([zlib.crc32(name.encode()), seed]).standard_normal(out[name].shape)
        drawn = base * np.exp(spread * noise) if base else spread * noise
        out[name] = jnp.asarray(drawn.astype(out[name].dtype))
    for name, factor in factors.items():
        out[name] = (out[name] * factor).astype(out[name].dtype)
    return out
```

```python
from contextlib import ExitStack

import concourse.bass as bass
from concourse import mybir

F32 = mybir.dt.float32
BF16 = mybir.dt.bfloat16
I32 = mybir.dt.int32
ALU = mybir.AluOpType
ACT = mybir.ActivationFunctionType
AX = mybir.AxisListType

P = 128
B = 64
E = 16
G = 5000
D = 128
HEADS = 8
DH = 64
INNER = HEADS * DH
HP = HEADS // 2
NX = 8
F = 512
FC = F // P
LN_EPS = 1e-5
NORM_FLOOR = 1e-12
SCALE = DH ** -0.5
A_FLOOR = 1e-10
INV_FLOOR = 1e-8

EH = E // 2
GT = G // P
GREM = G - GT * P
TC = 2
NCH = -(-(GT + 1) // TC)
SLOT = EH * TC * D
NSLOT = 5
UB = 16
NU = B // UB
NT = 2 * NU
NTOK = B * E
HTOK = NTOK // 2
TILES = NTOK // P + NX - 1
ROW = D + 4
NO_TOKEN = 4096.0

AHEAD = {"norm": 2, "gate0": 1, "gate1": 1, "values": 2, "pair0": 2, "pair1": 2, "pair2": 2, "pair3": 2,
         "project": 2, "route": 0}


def build(nc, x_t, weight, tok_bias, mask, gamma, w_qkv, bq, bk, b_v, w_a, ba, w_out, b_out,
          w_s, b_s, w1, b1, w2, b2, out):
    ctx = ExitStack()
    with ctx:
        def sb(name, shape, dt=F32):
            return ctx.enter_context(nc.sbuf_tensor(name, shape, dt))

        def sem(name):
            return ctx.enter_context(nc.semaphore(name))

        xT = sb("xT", [P, GT + 1, B])
        maskt = sb("maskt", [P, GT + 1, D])
        ring = sb("ring", [P, NSLOT, SLOT])
        flat = ring[:, :, :].rearrange("p a b -> p (a b)")
        w1_sb = flat[:, 0:NX * F]
        w2_sb = flat[:, NX * F:2 * NX * F]
        wqkv_sb = sb("wqkv_sb", [P, 3 * INNER])
        wa_sb = sb("wa_sb", [P, INNER])
        wout_sb = sb("wout_sb", [P, HP, D])
        gamma_sb = sb("gamma_sb", [P, 1])
        bq_sb = sb("bq_sb", [P, HP])
        bk_sb = sb("bk_sb", [P, HP])
        ba_sb = sb("ba_sb", [P, HP])
        nba_sb = sb("nba_sb", [P, HP])
        bv_bc = sb("bv_bc", [P, INNER])
        bout_bc = sb("bout_bc", [P, D])
        tokb_bc = sb("tokb_bc", [P, 2, NU * D])
        ws_sb = sb("ws_sb", [P, NX])
        bs_bc = sb("bs_bc", [P, NX])
        ident = sb("ident", [P, P])
        ones_bf = sb("ones_bf", [P, P], BF16)
        earlier = sb("earlier", [P, P], BF16)
        keep = sb("keep", [P, 2, P])
        restart = sb("restart", [P, 2 * HTOK], BF16)
        pow_half = sb("pow_half", [P, 4])
        rev = sb("rev", [P, NX])
        base = sb("base", [P, NX])
        steps = sb("steps", [P, NX])
        before = sb("before", [P, NX, NX])
        tile_no = sb("tile_no", [P, TILES])
        pidx = sb("pidx", [P, 1], I32)
        pidx8 = sb("pidx8", [P, 1], I32)
        pmod = sb("pmod", [P, 1], I32)
        pmod_f = sb("pmod_f", [P, 1])
        tok_f = sb("tok_f", [P, 2])
        token = sb("token", [P, NT])
        part = sb("part", [P, 4])
        zero_row = sb("zero_row", [P, ROW])
        hraw = sb("hraw", [P, NU, D])
        stats = sb("stats", [P, NU, 6])
        mv = sb("mv", [P, NU, 2])
        tiny = sb("tiny", [P, NU, 2])
        scale = sb("scale", [P, NU])
        xn = sb("xn", [P, NU, D])
        xnT = sb("xnT", [P, HTOK])
        gl = sb("gl", [P, HP, HTOK])
        cum = sb("cum", [P, HP, HTOK])
        ginv = sb("ginv", [P, HP, HTOK])
        kraw = sb("kraw", [P, HTOK])
        ks = sb("ks", [P, 2, HP, HTOK])
        qs = sb("qs", [P, 2, HTOK])
        vv = sb("vv", [P, 2, NU, INNER])
        att = sb("att", [P, 2, 2, HTOK])
        aoT = sb("aoT", [P, HP, HTOK])
        rows = sb("rows", [P, NT, ROW])
        xf = hraw
        xfT = xnT
        lg = sb("lg", [P, NU, NX])
        mx = sb("mx", [P, NU])
        cand = sb("cand", [P, NU, NX])
        cm = sb("cm", [P, NT])
        ex = sb("ex", [P, NU, NX])
        esum = sb("esum", [P, NU])
        oh = sb("oh", [P, NT, NX])
        ohb = sb("ohb", [P, NT, NX], BF16)
        rank = sb("rank", [P, NT, NX])
        cnt = sb("cnt", [P, NX])
        cmp = sb("cmp", [P, NX, NX])
        ntile = sb("ntile", [P, NX])
        first = sb("first", [P, NX])
        last = sb("last", [P, NX])
        slot_f = sb("slot_f", [P, NT])
        slot_i = sb("slot_i", [P, NT], I32)
        owner_c = sb("owner_c", [P, TILES, NX])
        owner_f = sb("owner_f", [P, TILES])
        owner_i = sb("owner_i", [P, TILES], I32)
        b12 = sb("b12", [3 * NX, F + D])
        b12r = sb("b12r", [3 * NX, F + D])
        b12p = [sb(f"b12p{i}", [3 * NX, F + D], BF16) for i in range(3)]
        b12b = sb("b12b", [3 * NX, F + D], BF16)
        pick = sb("pick", [3 * NX, TILES, P], BF16)
        srow = ks[:, :, :, :].rearrange("p a b c -> p (a b c)")[:, 0:TILES * ROW].rearrange("p (t r) -> p t r", r=ROW)
        sx = gl[:, 0, :].rearrange("p (a b) -> p a b", a=4)
        sxT = gl[:, 1, :].rearrange("p (a b) -> p a b", a=4)
        hid = cum[:, 0:2, :]
        hidT = cum[:, 2:4, :]
        fin = ginv[:, 0, :].rearrange("p (a b) -> p a b", a=4)
        fin0 = ginv[:, 1, :].rearrange("p (a b) -> p a b", a=4)
        dest_f = sb("dest_f", [P, TILES])
        dest = sb("dest", [P, TILES], I32)

        bank = [ctx.enter_context(nc.psum_tensor(f"bank{i}", [P, 512], F32)) for i in range(8)]
        h_rows = nc.dram_tensor("h_rows", [2, B, EH * D], F32, kind="Internal").ap()
        sorted_rows = nc.dram_tensor("sorted_rows", [TILES * P, ROW], F32, kind="Internal").ap()

        slot_in = [sem(f"slot_in{i}") for i in range(NSLOT)]
        x_in = sem("x_in")
        tokb_in = sem("tokb_in")
        attn_in = sem("attn_in")
        w1_in = sem("w1_in")
        w2_in = sem("w2_in")
        b12_in = sem("b12_in")
        h_out = sem("h_out")
        res_in = sem("res_in")
        zeroed = sem("zeroed")
        spread = sem("spread")
        srow_in = [sem(f"srow_in{i}") for i in range(4)]
        stored = [sem(f"stored{i}") for i in range(4)]
        const_pool = sem("const_pool")
        pool_step = sem("pool_step")
        dve_step = sem("dve_step")
        const_dve = sem("const_dve")
        masked = sem("masked")
        used = sem("used")
        raw_done = sem("raw_done")
        var_done = sem("var_done")
        scale_done = sem("scale_done")
        xn_done = sem("xn_done")
        xnT_ps = sem("xnT_ps")
        xnT_done = sem("xnT_done")
        gate_ps = sem("gate_ps")
        gate_exp = sem("gate_exp")
        gate_clip = sem("gate_clip")
        gate_ln = sem("gate_ln")
        gate_cum = sem("gate_cum")
        gate_cap = sem("gate_cap")
        gate_a = sem("gate_a")
        gate_inv = sem("gate_inv")
        v_ps = sem("v_ps")
        v_done = sem("v_done")
        k_ps = sem("k_ps")
        k_raw = sem("k_raw")
        k_done = sem("k_done")
        q_ps = sem("q_ps")
        q_done = sem("q_done")
        sim_ps = sem("sim_ps")
        att_done = sem("att_done")
        ao_ps = sem("ao_ps")
        ao_done = sem("ao_done")
        y_ps = sem("y_ps")
        h1_done = sem("h1_done")
        var2_done = sem("var2_done")
        scale2_done = sem("scale2_done")
        xf_done = sem("xf_done")
        xfT_ps = sem("xfT_ps")
        xfT_done = sem("xfT_done")
        lg_ps = sem("lg_ps")
        lm_done = sem("lm_done")
        ex_done = sem("ex_done")
        oh_done = sem("oh_done")
        rank_ps = sem("rank_ps")
        rank_done = sem("rank_done")
        cnt_ps = sem("cnt_ps")
        slot_done = sem("slot_done")
        owner_done = sem("owner_done")
        pick_done = sem("pick_done")
        sx_done = sem("sx_done")
        sxT_ps = sem("sxT_ps")
        sxT_done = sem("sxT_done")
        hid_ps = sem("hid_ps")
        hid_done = sem("hid_done")
        hidT_ps = sem("hidT_ps")
        hidT_done = sem("hidT_done")
        ffn_ps = sem("ffn_ps")
        fin0_done = sem("fin0_done")
        fin_done = sem("fin_done")
        dest_done = sem("dest_done")

        block = ctx.enter_context(nc.Block())

        def rows_of(c):
            return [(t, P if t < GT else GREM) for t in range(TC * c, min(TC * c + TC, GT + 1))]

        def slot_in_count(n):
            total = 0
            for m in range(n % NSLOT, n + 1, NSLOT):
                h, c = divmod(m, NCH)
                dmas = 2 if c == NCH - 1 else 1
                total += 16 * dmas * (2 if h == 0 else 1)
            return total

        def masked_count(n):
            return sum(3 if m % NCH == NCH - 1 else 2 for m in range(n + 1))

        def chunk_view(n):
            return ring[:, n % NSLOT, :].rearrange("p (e t d) -> p e t d", e=EH, t=TC)

        w_main = weight[:, 0:GT * P, :].rearrange("e (p t) d -> p e t d", t=GT)
        w_rest = weight[:, GT * P:G, :].rearrange("e p d -> p e d")
        m_main = mask[0:GT * P, :].rearrange("(p t) d -> p t d", t=GT)
        m_rest = mask[GT * P:G, :]
        x_main = x_t[0:GT * P, :].rearrange("(p t) b -> p t b", t=GT)
        x_rest = x_t[GT * P:G, :]

        class Ahead:

            def __init__(self):
                self.next = NCH

            def after(self, stage, half):
                n0 = self.next
                if half == 0:
                    count = AHEAD[stage] if stage != "route" else 2 * NCH - n0
                    self.next = min(2 * NCH, n0 + count)
                return range(n0, self.next)

        def sim_group(half, hp, key_half):
            return hp if half == 0 else HP + 2 * hp + key_half

        def group_reader(n):
            return n + 1 if n < HP else HP + (n - HP) // 2 + 1

        @block.sync
        def _(sp):
            def load_chunk(n):
                half, c = divmod(n, NCH)
                s = slot_in[n % NSLOT]
                if n >= NSLOT:
                    sp.wait_ge(used, n - NSLOT + 1)
                ts = [t for t, k in rows_of(c) if k == P]
                t0, t1 = ts[0], ts[-1] + 1
                v = chunk_view(n)
                if half == 0:
                    sp.dma_start(maskt[:, t0:t1, :], m_main[:, t0:t1, :]).then_inc(s, 16)
                sp.dma_start(v[:, :, 0:t1 - t0, :], w_main[:, half * EH:(half + 1) * EH, t0:t1, :]).then_inc(s, 16)
                if c == NCH - 1:
                    if half == 0:
                        sp.dma_start(maskt[0:GREM, GT, :], m_rest).then_inc(s, 16)
                    sp.dma_start(v[0:GREM, :, 1, :], w_rest[:, half * EH:(half + 1) * EH, :]).then_inc(s, 16)

            sp.dma_start(xT[:, 0:GT, :], x_main).then_inc(x_in, 16)
            sp.dma_start(xT[0:GREM, GT, :], x_rest).then_inc(x_in, 16)
            for n in range(2 * NCH):
                load_chunk(n)
                if n == NCH - 6:
                    for half in range(2):
                        for s in range(2):
                            e0 = half * EH + s * NU
                            src = tok_bias[e0:e0 + NU, :].rearrange("(a e) d -> a (e d)", a=1)
                            sp.dma_start(tokb_bc[s * B:(s + 1) * B, half, :],
                                         src.broadcast_to([B, NU * D])).then_inc(tokb_in, 16)
                    for dst, src in ((wa_sb[:], w_a), (wqkv_sb[:], w_qkv),
                                     (wout_sb[:], w_out.rearrange("(c p) d -> p c d", p=P)),
                                     (gamma_sb[:], gamma), (bq_sb[:], bq), (bk_sb[:], bk), (ba_sb[:], ba),
                                     (bv_bc[:], b_v.broadcast_to([P, INNER])),
                                     (bout_bc[:], b_out.broadcast_to([P, D])),
                                     (ws_sb[:], w_s), (bs_bc[:], b_s.broadcast_to([P, NX]))):
                        sp.dma_start(dst, src).then_inc(attn_in, 16)
                    for i in range(3):
                        sp.dma_start(b12[i * NX:(i + 1) * NX, 0:F], b1).then_inc(b12_in, 16)
                        sp.dma_start(b12[i * NX:(i + 1) * NX, F:F + D], b2).then_inc(b12_in, 16)
            sp.wait_ge(used, 2 * NCH)
            sp.dma_start(w1_sb.rearrange("p (e f) -> p e f", e=NX), w1.rearrange("e d f -> d e f")).then_inc(w1_in, 16)
            sp.dma_start(w2_sb.rearrange("p (e c d) -> p e c d", e=NX, c=FC),
                         w2.rearrange("e (c p) d -> p e c d", p=P)).then_inc(w2_in, 16)
            sp.wait_ge(spread, 16 * NT)
            sp.wait_ge(ao_ps, 2 * HP)
            for j in range(TILES):
                if j >= 4:
                    sp.wait_ge(srow_in[j % 4], 16 * (j // 4))
                sp.dma_start(srow[:, j, :], sorted_rows[j * P:(j + 1) * P, :]).then_inc(srow_in[j % 4], 16)

        @block.gpsimd
        def _(pool):
            count = [0]

            def link(ins):
                count[0] += 1
                ins.then_inc(pool_step, 1)
                pool.wait_ge(pool_step, count[0])

            link(nc.gpsimd.memset(ident[:], 0.0))
            nc.gpsimd.affine_select(out=ident[:], in_=ident[:], compare_op=ALU.not_equal, fill=1.0, base=0,
                                    pattern=[[-1, P]], channel_multiplier=1).then_inc(const_pool, 1)
            nc.gpsimd.memset(ones_bf[:], 1.0).then_inc(const_pool, 1)
            nc.gpsimd.memset(pow_half[:], -0.5).then_inc(const_pool, 1)
            link(nc.gpsimd.memset(earlier[:], 1.0))
            nc.gpsimd.affine_select(out=earlier[:], in_=earlier[:], compare_op=ALU.is_gt, fill=0.0, base=0,
                                    pattern=[[1, P]], channel_multiplier=-1).then_inc(const_pool, 1)
            link(nc.gpsimd.memset(keep[:], SCALE))
            for s in range(2):
                v = keep[:, s, :].rearrange("p (b e) -> p b e", e=EH)
                link(nc.gpsimd.affine_select(out=v, in_=v, compare_op=ALU.is_ge, fill=0.0, base=0,
                                             pattern=[[-EH, UB], [0, EH]], channel_multiplier=1))
                link(nc.gpsimd.affine_select(out=v, in_=v, compare_op=ALU.is_ge, fill=0.0, base=EH - 1,
                                             pattern=[[EH, UB], [0, EH]], channel_multiplier=-1))
            nc.gpsimd.affine_select(out=keep[:, 0, :], in_=keep[:, 0, :], compare_op=ALU.is_ge, fill=0.0, base=0,
                                    pattern=[[1, P]], channel_multiplier=-1).then_inc(const_pool, 1)
            link(nc.gpsimd.memset(restart[:], 1.0))
            nc.gpsimd.memset(restart[:].rearrange("p (b e) -> p b e", e=EH)[:, :, 0:1], 0.0).then_inc(const_pool, 1)
            small = dict(allow_small_or_imprecise_dtypes=True)
            nc.gpsimd.iota(rev[:], [[-1, NX]], base=NX, channel_multiplier=0, **small).then_inc(const_pool, 1)
            nc.gpsimd.iota(steps[:], [[P, NX]], base=0, channel_multiplier=0, **small).then_inc(const_pool, 1)
            nc.gpsimd.iota(tile_no[:], [[1, TILES]], base=0, channel_multiplier=0, **small).then_inc(const_pool, 1)
            nc.gpsimd.iota(pidx[:], [[0, 1]], base=0, channel_multiplier=1).then_inc(const_pool, 1)
            link(nc.gpsimd.memset(before[:], 1.0))
            nc.gpsimd.affine_select(out=before[:], in_=before[:], compare_op=ALU.is_gt, fill=0.0, base=0,
                                    pattern=[[1, NX], [-1, NX]], channel_multiplier=0).then_inc(const_pool, 1)
            link(nc.gpsimd.memset(part[:], 1.0))
            link(nc.gpsimd.affine_select(out=part[:, 0:3], in_=part[:, 0:3], compare_op=ALU.is_ge, fill=0.0, base=0,
                                         pattern=[[-NX, 3]], channel_multiplier=1))
            nc.gpsimd.affine_select(out=part[:, 0:3], in_=part[:, 0:3], compare_op=ALU.is_ge, fill=0.0, base=NX - 1,
                                    pattern=[[NX, 3]], channel_multiplier=-1).then_inc(const_pool, 1)
            link(nc.gpsimd.memset(zero_row[:], 0.0))
            pool.dma_start(sorted_rows.rearrange("(t p) r -> p t r", p=P),
                           zero_row[:].rearrange("p (a r) -> p a r", a=1).broadcast_to([P, TILES, ROW]))\
                .then_inc(zeroed, 16)

            for half in range(2):
                pool.wait_ge(var_done, half + 1)
                nc.gpsimd.tensor_tensor(scale[:], tiny[:, :, 1], pow_half[:], ALU.pow).then_inc(scale_done, 1)
                pool.wait_ge(raw_done, half + 1)
                for s in range(2):
                    pool.dma_start(h_rows[half, :, s * NU * D:(s + 1) * NU * D],
                                   hraw[s * B:(s + 1) * B, :, :].rearrange("p u d -> p (u d)")).then_inc(h_out, 16)
                pool.wait_ge(h_out, 32 * (half + 1))
                pool.dma_start(rows[:, half * NU:(half + 1) * NU, 0:D],
                               h_rows[half].rearrange("(u c) (e d) -> (c e) u d", c=UB, e=EH)).then_inc(res_in, 16)
                pool.wait_ge(var2_done, half + 1)
                nc.gpsimd.tensor_tensor(scale[:], tiny[:, :, 1], pow_half[:], ALU.pow).then_inc(scale2_done, 1)
            pool.wait_ge(slot_done, 1)
            pool.wait_ge(zeroed, 16)
            for t in range(NT):
                pool.indirect_dma_start(out=sorted_rows, out_offset=bass.IndirectOffsetOnAxis(ap=slot_i[:, t:t + 1], axis=0),
                                        in_=rows[:, t, :], in_offset=None).then_inc(spread, 16)
            pool.wait_ge(dest_done, 1)
            out_rows = out.rearrange("b e d -> (b e) d")
            for j in range(TILES):
                pool.wait_ge(fin_done, j + 1)
                pool.indirect_dma_start(out=out_rows, out_offset=bass.IndirectOffsetOnAxis(ap=dest[:, j:j + 1], axis=0),
                                        in_=fin[:, j % 4, :], in_offset=None,
                                        bounds_check=NTOK - 1, oob_is_err=False).then_inc(stored[j % 4], 16)
            for k in range(4):
                pool.wait_ge(stored[k], 16 * len(range(k, TILES, 4)))

        @block.scalar
        def _(act):
            act.wait_ge(attn_in, 16 * 11)
            act.wait_ge(const_dve, 1)
            for half in range(2):
                act.wait_ge(xnT_ps, half + 1)
                if half:
                    act.wait_ge(lg_ps, half)
                nc.scalar.activation(xnT[:].rearrange("p (b s e) -> p e s b", s=2, e=NU),
                                     bank[1][:].rearrange("p (e s b) -> p e s b", s=2, b=B),
                                     ACT.Copy, scale=gamma_sb[:, 0:1]).then_inc(xnT_done, 1)
                for hp in range(HP):
                    act.wait_ge(gate_ps, half * HP + hp + 1)
                    if half and hp == 0:
                        act.wait_ge(q_done, HP)
                    nc.scalar.activation(gl[:, hp, :], bank[4 + hp][:], ACT.Exp, scale=-1.0,
                                         bias=nba_sb[:, hp:hp + 1]).then_inc(gate_exp, 1)
                for g in range(2):
                    act.wait_ge(gate_clip, 2 * half + g + 1)
                    nc.scalar.activation(gl[:, 2 * g:2 * g + 2, :], gl[:, 2 * g:2 * g + 2, :], ACT.Ln)\
                        .then_inc(gate_ln, 1)
                for g in range(2):
                    act.wait_ge(gate_cum, 2 * half + g + 1)
                    nc.scalar.activation(gl[:, 2 * g:2 * g + 2, :], cum[:, 2 * g:2 * g + 2, :], ACT.Exp, scale=-1.0)\
                        .then_inc(gate_a, 1)
                    act.wait_ge(gate_cap, 2 * half + g + 1)
                    nc.scalar.activation(ginv[:, 2 * g:2 * g + 2, :], ginv[:, 2 * g:2 * g + 2, :], ACT.Exp)\
                        .then_inc(gate_inv, 1)
                def key_bias(hp):
                    i = half * HP + hp
                    act.wait_ge(k_ps, i + 1)
                    if i:
                        act.wait_ge(k_done, i)
                    nc.scalar.activation(kraw[:], bank[2][:], ACT.Identity, bias=bk_sb[:, hp:hp + 1]).then_inc(k_raw, 1)

                key_bias(0)
                for hp in range(HP):
                    if hp + 1 < HP:
                        key_bias(hp + 1)
                    i = half * HP + hp
                    act.wait_ge(ao_ps, i + 1)
                    if half and hp == 0:
                        act.wait_ge(y_ps, half)
                    nc.scalar.activation(aoT[:, hp, :], bank[1][:], ACT.Copy).then_inc(ao_done, 1)
                act.wait_ge(xfT_ps, half + 1)
                nc.scalar.activation(xfT[:], bank[1][:], ACT.Copy).then_inc(xfT_done, 1)
                act.wait_ge(lm_done, half + 1)
                nc.scalar.activation(ex[:], lg[:], ACT.Exp).then_inc(ex_done, 1)
            for j in range(TILES):
                act.wait_ge(hid_ps, j + 1)
                if j >= 2:
                    act.wait_ge(hidT_ps, j - 1)
                nc.scalar.activation(hid[:, j % 2, :], bank[2 + j % 2][:], ACT.Gelu).then_inc(hid_done, 1)

        @block.vector
        def _(dve):
            count = [0]
            ahead = Ahead()

            def link(ins):
                count[0] += 1
                ins.then_inc(dve_step, 1)
                dve.wait_ge(dve_step, count[0])

            def mask_chunk(n):
                half, c = divmod(n, NCH)
                dve.wait_ge(slot_in[n % NSLOT], slot_in_count(n))
                v = chunk_view(n)
                ts = [t for t, k in rows_of(c) if k == P]
                t0, w = ts[0], len(ts)
                for s in range(2):
                    part_v = v[:, s * NU:(s + 1) * NU, 0:w, :]
                    m = maskt[:, t0:t0 + w, :].rearrange("p (a t) d -> p a t d", a=1).broadcast_to([P, NU, w, D])
                    nc.vector.tensor_tensor(part_v, part_v, m, ALU.mult).then_inc(masked, 1)
                if c == NCH - 1:
                    part_v = v[0:GREM, :, 1, :]
                    m = maskt[0:GREM, GT:GT + 1, :].broadcast_to([GREM, EH, D])
                    nc.vector.tensor_tensor(part_v, part_v, m, ALU.mult).then_inc(masked, 1)

            def moments(src, s6, var_sem_step):
                for u in range(NU):
                    ins = nc.vector.bn_stats(s6[:, u, :], src(u))
                    if u == NU - 1:
                        link(ins)
                    else:
                        ins.then_inc(dve_step, 1)
                        count[0] += 1
                for u in range(NU):
                    ins = nc.vector.bn_aggr(mv[:, u, :], s6[:, u, :])
                    if u == NU - 1:
                        link(ins)
                    else:
                        ins.then_inc(dve_step, 1)
                        count[0] += 1

            for n in range(NCH):
                if n == 3:
                    dve.wait_ge(const_pool, 12)
                    link(nc.vector.tensor_single_scalar(pidx8[:], pidx[:], -EH, ALU.bitwise_and))
                    link(nc.vector.tensor_single_scalar(pmod[:], pidx[:], NX - 1, ALU.bitwise_and))
                    link(nc.vector.tensor_copy(pmod_f[:], pmod[:]))
                    link(nc.vector.tensor_copy(tok_f[:, 0:1], pidx[:]))
                    link(nc.vector.tensor_copy(tok_f[:, 1:2], pidx8[:]))
                    link(nc.vector.tensor_tensor(tok_f[:, 0:1], tok_f[:, 0:1], tok_f[:, 1:2], ALU.add))
                    for t in range(NT):
                        half, u = divmod(t, NU)
                        link(nc.vector.tensor_scalar_add(rows[:, t, D + 3:D + 4], tok_f[:, 0:1],
                                                         float(u * UB * E + half * EH) - NO_TOKEN))
                mask_chunk(n)
            dve.wait_ge(attn_in, 16 * 11)
            nc.vector.tensor_scalar_mul(nba_sb[:], ba_sb[:], -1.0).then_inc(const_dve, 1)
            dve.wait_ge(b12_in, 16 * 6)
            link(nc.vector.tensor_copy(b12p[0][:], b12[:]))
            link(nc.vector.tensor_tensor(b12r[:], b12[:], b12p[0][:], ALU.subtract))
            link(nc.vector.tensor_copy(b12p[1][:], b12r[:]))
            link(nc.vector.tensor_tensor(b12p[2][:], b12r[:], b12p[1][:], ALU.subtract))
            link(nc.vector.tensor_scalar(b12r[:], b12p[0][:], part[0:3 * NX, 0:1], None, ALU.mult))
            for i in (1, 2):
                link(nc.vector.scalar_tensor_tensor(b12r[:], b12p[i][:], part[0:3 * NX, i:i + 1], b12r[:],
                                                    ALU.mult, ALU.add))
            link(nc.vector.tensor_copy(b12b[:], b12r[:]))
            dve.wait_ge(tokb_in, 16 * 4)

            for half in range(2):
                def after(stage):
                    for n in ahead.after(stage, half):
                        mask_chunk(n)

                dve.wait_ge(used, NCH * (half + 1))
                nc.vector.tensor_tensor(hraw[:].rearrange("p u d -> p (u d)"), bank[0][:], tokb_bc[:, half, :],
                                        ALU.add).then_inc(raw_done, 1)
                dve.wait_ge(raw_done, half + 1)
                moments(lambda u: hraw[:, u, :], stats, None)
                floor = NORM_FLOOR ** 2 / D
                link(nc.vector.tensor_scalar(tiny[:, :, 0], mv[:, :, 1], LN_EPS, floor, ALU.add, ALU.mult))
                nc.vector.tensor_tensor(tiny[:, :, 1], mv[:, :, 1], tiny[:, :, 0], ALU.max).then_inc(var_done, 1)
                dve.wait_ge(scale_done, half + 1)
                for u in range(NU):
                    nc.vector.tensor_scalar(xn[:, u, :], hraw[:, u, :], mv[:, u, 0:1], scale[:, u:u + 1],
                                            ALU.subtract, ALU.mult).then_inc(xn_done, 1)
                after("norm")
                for g in range(2):
                    gs = gl[:, 2 * g:2 * g + 2, :]
                    cs = cum[:, 2 * g:2 * g + 2, :]
                    dve.wait_ge(gate_exp, half * HP + 2 * g + 2)
                    nc.vector.tensor_scalar(gs, gs, 1.0, 1.0 / A_FLOOR, ALU.add, ALU.min).then_inc(gate_clip, 1)
                for g in range(2):
                    gs = gl[:, 2 * g:2 * g + 2, :]
                    cs = cum[:, 2 * g:2 * g + 2, :]
                    dve.wait_ge(gate_ln, 2 * half + g + 1)
                    if half:
                        gv = gs.rearrange("p c (b e) -> p c b e", e=EH)[:, :, :, 0]
                        cv = cs.rearrange("p c (b e) -> p c b e", e=EH)[:, :, :, EH - 1]
                        dve.wait_ge(gate_cum, 2)
                        link(nc.vector.tensor_tensor(gv, gv, cv, ALU.add))
                        dve.wait_ge(gate_a, 2)
                    nc.vector.tensor_tensor_scan(cs.rearrange("p c t -> p (c t)"), restart[:],
                                                 gs.rearrange("p c t -> p (c t)"), 0.0, ALU.mult, ALU.add)\
                        .then_inc(gate_cum, 1)
                    dve.wait_ge(gate_cum, 2 * half + g + 1)
                    if half:
                        dve.wait_ge(k_done, HP)
                    nc.vector.tensor_scalar_min(ginv[:, 2 * g:2 * g + 2, :], cs, 40.0).then_inc(gate_cap, 1)
                    after(f"gate{g}")
                for u in range(NU):
                    dve.wait_ge(v_ps, half * NU + u + 1)
                    nc.vector.tensor_tensor(vv[:, half, u, :], bank[2 + u % 2][:], bv_bc[:], ALU.add).then_inc(v_done, 1)
                after("values")

                def scaled_key_query(hp):
                    i = half * HP + hp
                    dve.wait_ge(k_raw, i + 1)
                    dve.wait_ge(gate_inv, 2 * half + hp // 2 + 1)
                    nc.vector.scalar_tensor_tensor(ks[:, half, hp, :], ginv[:, hp, :], 1.0 / INV_FLOOR, kraw[:],
                                                   ALU.min, ALU.mult).then_inc(k_done, 1)
                    dve.wait_ge(q_ps, i + 1)
                    if i >= 2:
                        dve.wait_ge(sim_ps, sim_group((i - 2) // HP, (i - 2) % HP, (i - 2) // HP) + 1)
                    nc.vector.scalar_tensor_tensor(qs[:, i % 2, :], bank[3][:], bq_sb[:, hp:hp + 1], gl[:, hp, :],
                                                   ALU.add, ALU.mult).then_inc(q_done, 1)

                def mask_scores(hp):
                    for key_half in range(half + 1):
                        n = sim_group(half, hp, key_half)
                        dve.wait_ge(sim_ps, n + 1)
                        if n >= 2:
                            dve.wait_ge(ao_ps, group_reader(n - 2))
                        m = keep[:, int(key_half < half), :].rearrange("p (a i) -> p a i", a=1).broadcast_to([P, NU, P])
                        for odd in range(2):
                            nc.vector.tensor_tensor(att[:, n % 2, odd, :].rearrange("p (u i) -> p u i", u=NU),
                                                    bank[4 + 2 * (n % 2) + odd][:].rearrange("p (u i) -> p u i", u=NU),
                                                    m, ALU.mult).then_inc(att_done, 1)

                scaled_key_query(0)
                for hp in range(HP):
                    if hp + 1 < HP:
                        scaled_key_query(hp + 1)
                    mask_scores(hp)
                    after(f"pair{hp}")

                h1 = rows[:, half * NU:(half + 1) * NU, 0:D]
                dve.wait_ge(res_in, 16 * (half + 1))
                link(nc.vector.tensor_tensor(h1, h1, bout_bc[:].rearrange("p (a d) -> p a d", a=1)
                                             .broadcast_to([P, NU, D]), ALU.add))
                dve.wait_ge(y_ps, half + 1)
                nc.vector.tensor_tensor(h1, h1, bank[2][:].rearrange("p (u d) -> p u d", u=NU), ALU.add)\
                    .then_inc(h1_done, 1)
                dve.wait_ge(h1_done, half + 1)
                after("project")
                moments(lambda u: rows[:, half * NU + u, 0:D], stats, None)
                link(nc.vector.tensor_copy(rows[:, half * NU:(half + 1) * NU, D], mv[:, :, 0]))
                nc.vector.tensor_scalar_add(tiny[:, :, 1], mv[:, :, 1], LN_EPS).then_inc(var2_done, 1)
                dve.wait_ge(scale2_done, half + 1)
                link(nc.vector.tensor_copy(rows[:, half * NU:(half + 1) * NU, D + 1], scale[:]))
                dve.wait_ge(res_in, 16 * (half + 1))
                for u in range(NU):
                    nc.vector.tensor_scalar(xf[:, u, :], rows[:, half * NU + u, 0:D], mv[:, u, 0:1],
                                            scale[:, u:u + 1], ALU.subtract, ALU.mult).then_inc(xf_done, 1)
                dve.wait_ge(lg_ps, half + 1)
                tiles = slice(half * NU, (half + 1) * NU)

                def over_x(ap):
                    return ap.rearrange("p (u a) -> p u a", a=1).broadcast_to([P, NU, NX])

                def over_u(ap):
                    return ap.rearrange("p (a x) -> p a x", a=1).broadcast_to([P, NU, NX])

                if half:
                    dve.wait_ge(ex_done, half)
                link(nc.vector.tensor_tensor(lg[:], bank[3][:, 0:NU * NX].rearrange("p (u x) -> p u x", u=NU),
                                             over_u(bs_bc[:]), ALU.add))
                link(nc.vector.tensor_reduce(mx[:], lg[:], AX.X, ALU.max))
                nc.vector.tensor_tensor(lg[:], lg[:], over_x(mx[:]), ALU.subtract).then_inc(lm_done, 1)
                dve.wait_ge(lm_done, half + 1)
                link(nc.vector.scalar_tensor_tensor(cand[:], lg[:], 0.0, over_u(rev[:]), ALU.is_ge, ALU.mult))
                link(nc.vector.tensor_reduce(cm[:, tiles], cand[:], AX.X, ALU.max))
                link(nc.vector.tensor_tensor(oh[:, tiles, :], cand[:], over_x(cm[:, tiles]), ALU.is_equal))
                nc.vector.tensor_copy(ohb[:, tiles, :], oh[:, tiles, :]).then_inc(oh_done, 1)
                dve.wait_ge(ex_done, half + 1)
                link(nc.vector.tensor_reduce(esum[:], ex[:], AX.X, ALU.add))
                link(nc.vector.reciprocal(rows[:, tiles, D + 2], esum[:]))
                after("route")

            def over_t(ap):
                return ap.rearrange("p (a x) -> p a x", a=1).broadcast_to([P, NT, NX])

            dve.wait_ge(rank_ps, 1)
            link(nc.vector.tensor_copy(cnt[:], bank[2][:, 0:NX]))
            link(nc.vector.tensor_tensor(cmp[:], cnt[:].rearrange("p (x a) -> p x a", a=1).broadcast_to([P, NX, NX]),
                                         steps[:].rearrange("p (a k) -> p a k", a=1).broadcast_to([P, NX, NX]), ALU.is_gt))
            link(nc.vector.tensor_reduce(ntile[:], cmp[:], AX.X, ALU.add))
            link(nc.vector.tensor_tensor(cmp[:], before[:],
                                         ntile[:].rearrange("p (a k) -> p a k", a=1).broadcast_to([P, NX, NX]), ALU.mult))
            link(nc.vector.tensor_reduce(first[:], cmp[:], AX.X, ALU.add))
            link(nc.vector.tensor_scalar_mul(base[:], first[:], float(P)))
            link(nc.vector.tensor_tensor(rank[:], bank[3][:, 0:NT * NX].rearrange("p (t x) -> p t x", t=NT),
                                         over_t(base[:]), ALU.add))
            link(nc.vector.tensor_tensor(rank[:], rank[:], oh[:], ALU.mult))
            link(nc.vector.tensor_reduce(slot_f[:], rank[:], AX.X, ALU.add))
            nc.vector.tensor_copy(slot_i[:], slot_f[:]).then_inc(slot_done, 1)
            link(nc.vector.tensor_tensor(last[:], first[:], ntile[:], ALU.add))
            link(nc.vector.tensor_tensor(owner_c[:], tile_no[:].rearrange("p (t a) -> p t a", a=1).broadcast_to([P, TILES, NX]),
                                         last[:].rearrange("p (a x) -> p a x", a=1).broadcast_to([P, TILES, NX]), ALU.is_ge))
            link(nc.vector.tensor_reduce(owner_f[:], owner_c[:], AX.X, ALU.add))
            link(nc.vector.tensor_scalar_min(owner_f[:], owner_f[:], float(NX - 1)))
            nc.vector.tensor_copy(owner_i[:], owner_f[:]).then_inc(owner_done, 1)
            nc.vector.tensor_scalar(pick[:], owner_f[0:3 * NX, :].rearrange("p (t a) -> p t a", a=1)
                                    .broadcast_to([3 * NX, TILES, P]), pmod_f[0:3 * NX, 0:1], None, ALU.is_equal)\
                .then_inc(pick_done, 1)

            def normalise(j):
                dve.wait_ge(srow_in[j % 4], 16 * (j // 4 + 1))
                if j >= 4:
                    dve.wait_ge(sxT_ps, j - 3)
                nc.vector.tensor_scalar(sx[:, j % 4, :], srow[:, j, 0:D], srow[:, j, D:D + 1], srow[:, j, D + 1:D + 2],
                                        ALU.subtract, ALU.mult).then_inc(sx_done, 1)

            def take_xT(j):
                dve.wait_ge(sxT_ps, j + 1)
                if j >= 4:
                    dve.wait_ge(hid_ps, j - 3)
                nc.vector.tensor_copy(sxT[:, j % 4, :], bank[1][:, 0:P]).then_inc(sxT_done, 1)

            def take_hidT(j):
                dve.wait_ge(hidT_ps, j + 1)
                if j >= 2:
                    dve.wait_ge(ffn_ps, j - 1)
                nc.vector.tensor_copy(hidT[:, j % 2, :], bank[4 + j % 2][:]).then_inc(hidT_done, 1)

            def finish(j):
                dve.wait_ge(ffn_ps, j + 1)
                if j >= 4:
                    dve.wait_ge(stored[j % 4], 16 * (j // 4))
                nc.vector.scalar_tensor_tensor(fin[:, j % 4, :], bank[6 + j % 2][:, 0:D], srow[:, j, D + 2:D + 3],
                                               srow[:, j, 0:D], ALU.mult, ALU.add).then_inc(fin_done, 1)

            for j in range(TILES + 2):
                if j < TILES:
                    normalise(j)
                    take_xT(j)
                if j == 1:
                    for k in range(4):
                        n_k = (TILES - 1 - k) // 4 + 1
                        dve.wait_ge(srow_in[k], 16 * n_k)
                    link(nc.vector.tensor_scalar_add(dest_f[:], srow[:, :, D + 3], NO_TOKEN))
                    nc.vector.tensor_copy(dest[:], dest_f[:]).then_inc(dest_done, 1)
                if 1 <= j < TILES + 1:
                    take_hidT(j - 1)
                if j >= 2:
                    finish(j - 2)

        @block.tensor
        def _(pe):
            ahead = Ahead()

            def multiply_chunk(n):
                half, c = divmod(n, NCH)
                if n == NCH:
                    pe.wait_ge(raw_done, 1)
                pe.wait_ge(masked, masked_count(n))
                v = chunk_view(n)
                for i, (t, k) in enumerate(rows_of(c)):
                    for s in range(2):
                        mm = nc.tensor.matmul(bank[0][s * B:(s + 1) * B, :], xT[0:k, t, :],
                                              v[0:k, s * NU:(s + 1) * NU, i, :],
                                              start=(t == 0), stop=(t == GT), tile_position=(0, s * B))
                mm.then_inc(used, 1)

            pe.wait_ge(x_in, 32)
            for n in range(NCH):
                multiply_chunk(n)
            pe.wait_ge(const_pool, 12)
            pe.wait_ge(attn_in, 16 * 11)

            for half in range(2):
                def after(stage):
                    for n in ahead.after(stage, half):
                        multiply_chunk(n)

                if half:
                    pe.wait_ge(xfT_done, half)
                for u in range(NU):
                    pe.wait_ge(xn_done, half * NU + u + 1)
                    mm = nc.tensor.transpose(bank[1][:, u * P:(u + 1) * P], xn[:, u, :], ident[:])
                mm.then_inc(xnT_ps, 1)
                after("norm")
                pe.wait_ge(xnT_done, half + 1)
                if half:
                    pe.wait_ge(att_done, 2 * HP)
                for hp in range(HP):
                    nc.tensor.matmul(bank[4 + hp][:], wa_sb[:, hp * P:(hp + 1) * P], xnT[:], start=True, stop=True)\
                        .then_inc(gate_ps, 1)
                after("gate0")
                after("gate1")
                for u in range(NU):
                    i = half * NU + u
                    if u >= 2:
                        pe.wait_ge(v_done, i - 1)
                    elif half:
                        pe.wait_ge(h1_done if u == 0 else lm_done, half)
                    nc.tensor.matmul(bank[2 + u % 2][:], xnT[:, u * P:(u + 1) * P], wqkv_sb[:, 2 * INNER:3 * INNER],
                                     start=True, stop=True).then_inc(v_ps, 1)
                after("values")

                def keys_queries(hp):
                    i = half * HP + hp
                    if hp == 0:
                        pe.wait_ge(v_done, (half + 1) * NU)
                    else:
                        pe.wait_ge(k_raw, i)
                    nc.tensor.matmul(bank[2][:], wqkv_sb[:, INNER + hp * P:INNER + (hp + 1) * P], xnT[:],
                                     start=True, stop=True).then_inc(k_ps, 1)
                    if hp:
                        pe.wait_ge(q_done, i)
                    nc.tensor.matmul(bank[3][:], wqkv_sb[:, hp * P:(hp + 1) * P], xnT[:],
                                     start=True, stop=True).then_inc(q_ps, 1)

                def scores(hp):
                    i = half * HP + hp
                    pe.wait_ge(k_done, i + 1)
                    pe.wait_ge(q_done, i + 1)
                    for key_half in range(half + 1):
                        n = sim_group(half, hp, key_half)
                        pe.wait_ge(gate_exp, HP * (half + 1))
                        if n >= 2:
                            pe.wait_ge(att_done, 2 * (n - 1))
                        for u in range(NU):
                            for odd in range(2):
                                r = slice(odd * DH, (odd + 1) * DH)
                                mm = nc.tensor.matmul(bank[4 + 2 * (n % 2) + odd][:, u * P:(u + 1) * P],
                                                      ks[r, key_half, hp, u * P:(u + 1) * P],
                                                      qs[r, i % 2, u * P:(u + 1) * P],
                                                      start=True, stop=True, tile_position=(odd * DH, 0))
                        mm.then_inc(sim_ps, 1)

                def mix(hp):
                    i = half * HP + hp
                    if hp == 0:
                        pe.wait_ge(xnT_done, half + 1)
                    else:
                        pe.wait_ge(ao_done, i)
                    pe.wait_ge(att_done, 2 * (sim_group(half, hp, half) + 1))
                    for u in range(NU):
                        for key_half in range(half + 1):
                            n = sim_group(half, hp, key_half)
                            for odd in range(2):
                                h = 2 * hp + odd
                                mm = nc.tensor.matmul(bank[1][odd * DH:(odd + 1) * DH, u * P:(u + 1) * P],
                                                      vv[:, key_half, u, h * DH:(h + 1) * DH],
                                                      att[:, n % 2, odd, u * P:(u + 1) * P],
                                                      start=(key_half == 0), stop=(key_half == half),
                                                      tile_position=(0, odd * DH))
                    mm.then_inc(ao_ps, 1)

                keys_queries(0)
                for hp in range(HP):
                    scores(hp)
                    if hp + 1 < HP:
                        keys_queries(hp + 1)
                    mix(hp)
                    after(f"pair{hp}")
                pe.wait_ge(ao_done, HP * (half + 1))
                for u in range(NU):
                    for hp in range(HP):
                        mm = nc.tensor.matmul(bank[2][:, u * P:(u + 1) * P], aoT[:, hp, u * P:(u + 1) * P],
                                              wout_sb[:, hp, :], start=(hp == 0), stop=(hp == HP - 1))
                mm.then_inc(y_ps, 1)
                after("project")
                for u in range(NU):
                    pe.wait_ge(xf_done, half * NU + u + 1)
                    mm = nc.tensor.transpose(bank[1][:, u * P:(u + 1) * P], xf[:, u, :], ident[:])
                mm.then_inc(xfT_ps, 1)
                pe.wait_ge(xfT_done, half + 1)
                for u in range(NU):
                    mm = nc.tensor.matmul(bank[3][:, u * NX:(u + 1) * NX], xfT[:, u * P:(u + 1) * P], ws_sb[:],
                                          start=True, stop=True)
                mm.then_inc(lg_ps, 1)
                after("route")

            pe.wait_ge(oh_done, 2)
            for t in range(NT):
                nc.tensor.matmul(bank[2][:, 0:NX], ones_bf[:], ohb[:, t, :], start=(t == 0), stop=(t == NT - 1))
            ohf = ohb[:].rearrange("p t x -> p (t x)")
            mm = nc.tensor.matmul(bank[3][:, 0:NT * NX], earlier[:], ohf, start=True, stop=False)
            for k in range(1, NT):
                mm = nc.tensor.matmul(bank[3][:, k * NX:NT * NX], ones_bf[:], ohf[:, 0:(NT - k) * NX],
                                      start=False, stop=(k == NT - 1))
            mm.then_inc(rank_ps, 1)

            pe.wait_ge(owner_done, 1)
            owner = [None] * TILES
            pe.wait_ge(pick_done, 1)

            def transpose_rows(j):
                pe.wait_ge(sx_done, j + 1)
                if j:
                    pe.wait_ge(sxT_done, j)
                nc.tensor.transpose(bank[1][:, 0:P], sx[:, j % 4, :], ident[:]).then_inc(sxT_ps, 1)

            def expand(j):
                owner[j] = pe.value_load(owner_i[0:1, j:j + 1], min_val=0, max_val=NX - 1)
                pe.wait_ge(sxT_done, j + 1)
                if j >= 2:
                    pe.wait_ge(hid_done, j - 1)
                o = bank[2 + j % 2][:]
                nc.tensor.matmul(o, sxT[:, j % 4, :], w1_sb[:, bass.ds(owner[j] * F, F)], start=True, stop=False)
                nc.tensor.matmul(o, pick[:, j, :], b12b[:, 0:F], start=False, stop=True).then_inc(hid_ps, 1)

            def turn(j):
                pe.wait_ge(hid_done, j + 1)
                if j >= 2:
                    pe.wait_ge(hidT_done, j - 1)
                for c in range(FC):
                    mm = nc.tensor.transpose(bank[4 + j % 2][:, c * P:(c + 1) * P], hid[:, j % 2, c * P:(c + 1) * P],
                                             ident[:])
                mm.then_inc(hidT_ps, 1)

            def contract(j):
                pe.wait_ge(hidT_done, j + 1)
                if j >= 2:
                    pe.wait_ge(fin_done, j - 1)
                o = bank[6 + j % 2][:, 0:D]
                nc.tensor.matmul(o, pick[:, j, :], b12b[:, F:F + D], start=True, stop=False)
                for c in range(FC):
                    mm = nc.tensor.matmul(o, hidT[:, j % 2, c * P:(c + 1) * P],
                                          w2_sb[:, bass.ds(owner[j] * F + c * D, D)], start=False, stop=(c == FC - 1))
                mm.then_inc(ffn_ps, 1)

            pe.wait_ge(w1_in, 16)
            pe.wait_ge(w2_in, 16)
            transpose_rows(0)
            for j in range(TILES + 1):
                if j < TILES:
                    expand(j)
                if j + 1 < TILES:
                    transpose_rows(j + 1)
                if j >= 1:
                    contract(j - 1)
                if j < TILES:
                    turn(j)


def kernel(x, L0_tok_weight, L0_tok_bias, L0_tok_mask, L0_attn_gamma, L0_attn_w_qkv, L0_attn_b_qkv, L0_attn_w_a,
           L0_attn_b_a, L0_attn_w_out, L0_attn_b_out, L0_ffn_Ws, L0_ffn_bs, L0_ffn_W1, L0_ffn_b1, L0_ffn_W2,
           L0_ffn_b2):
    import numpy as np
    import concourse.bacc as bacc
    from concourse.bass_utils import run_bass_kernel_spmd

    def by_partition(v):
        return np.ascontiguousarray(np.asarray(v).reshape(-1, P).T)

    bqkv = np.asarray(L0_attn_b_qkv)
    arrays = {
        "x_t": np.ascontiguousarray(np.asarray(x).T),
        "weight": np.asarray(L0_tok_weight),
        "tok_bias": np.asarray(L0_tok_bias),
        "mask": np.asarray(L0_tok_mask),
        "gamma": by_partition(L0_attn_gamma),
        "w_qkv": np.asarray(L0_attn_w_qkv),
        "bq": by_partition(bqkv[0:INNER]),
        "bk": by_partition(bqkv[INNER:2 * INNER]),
        "b_v": bqkv[2 * INNER:3 * INNER].reshape(1, INNER),
        "w_a": np.asarray(L0_attn_w_a),
        "ba": by_partition(L0_attn_b_a),
        "w_out": np.asarray(L0_attn_w_out),
        "b_out": np.asarray(L0_attn_b_out).reshape(1, D),
        "w_s": np.asarray(L0_ffn_Ws),
        "b_s": np.asarray(L0_ffn_bs).reshape(1, NX),
        "w1": np.asarray(L0_ffn_W1),
        "b1": np.asarray(L0_ffn_b1),
        "w2": np.asarray(L0_ffn_W2),
        "b2": np.asarray(L0_ffn_b2),
    }
    nc = bacc.Bacc("TRN2", target_bir_lowering=False, num_devices=1)
    feeds, aps = {}, {}
    for name, a in arrays.items():
        feeds[f"in_{name}"] = np.ascontiguousarray(a)
        aps[name] = nc.dram_tensor(f"in_{name}", a.shape, mybir.dt.from_np(a.dtype), kind="ExternalInput").ap()
    aps["out"] = nc.dram_tensor("out_tower", (B, E, D), F32, kind="ExternalOutput").ap()
    build(nc, **aps)
    r = run_bass_kernel_spmd(nc, [feeds], core_ids=[0])
    return r.results[0]["out_tower"]
```

```python
from contextlib import ExitStack

import concourse.bass as bass
from concourse import mybir

F32 = mybir.dt.float32
BF16 = mybir.dt.bfloat16
I32 = mybir.dt.int32
ALU = mybir.AluOpType
ACT = mybir.ActivationFunctionType
AX = mybir.AxisListType

P = 128
B = 64
E = 16
G = 5000
D = 128
HEADS = 8
DH = 64
INNER = HEADS * DH
HP = HEADS // 2
NX = 8
F = 512
FC = F // P
LN_EPS = 1e-5
NORM_FLOOR = 1e-12
SCALE = DH ** -0.5
A_FLOOR = 1e-10
INV_FLOOR = 1e-8

EH = E // 2
GT = G // P
GREM = G - GT * P
TC = 2
NCH = -(-(GT + 1) // TC)
SLOT = EH * TC * D
NSLOT = 5
UB = 16
NU = B // UB
NT = 2 * NU
NTOK = B * E
HTOK = NTOK // 2
TILES = NTOK // P + NX - 1
ROW = D + 4
NCONST = 14
NO_TOKEN = 4096.0

AHEAD = {"norm": 2, "gates": 3, "values": 2, "first": 2, "pair0": 2, "pair1": 2, "pair2": 2, "pair3": 1,
         "project": 2}
LEAD = 2
B1 = slice(0, F)
B2 = slice(F, F + D)
BV = slice(F + D, F + D + INNER)
BO = slice(F + D + INNER, F + D + INNER + D)
NBIAS = F + D + INNER + D


def build(nc, x_t, weight, tok_bias, mask, gamma, w_qkv, bq, bk, b_v, w_a, ba, w_out, b_out,
          w_s, b_s, w1, b1, w2, b2, out):
    ctx = ExitStack()
    with ctx:
        def sb(name, shape, dt=F32):
            return ctx.enter_context(nc.sbuf_tensor(name, shape, dt))

        def sem(name):
            return ctx.enter_context(nc.semaphore(name))

        xT = sb("xT", [P, GT + 1, B])
        maskt = sb("maskt", [P, GT + 1, D])
        ring = sb("ring", [P, NSLOT, SLOT])
        flat = ring[:, :, :].rearrange("p a b -> p (a b)")
        w1_sb = flat[:, 0:NX * F]
        w2_sb = flat[:, NX * F:2 * NX * F]
        wqkv_sb = sb("wqkv_sb", [P, 3 * INNER])
        wa_sb = sb("wa_sb", [P, INNER])
        wout_sb = sb("wout_sb", [P, HP, D])
        gamma_sb = sb("gamma_sb", [P, 1])
        bq_sb = sb("bq_sb", [P, HP])
        bk_sb = sb("bk_sb", [P, HP])
        ba_sb = sb("ba_sb", [P, HP])
        nba_sb = sb("nba_sb", [P, HP])
        tokb_bc = sb("tokb_bc", [P, 2, NU * D])
        ws_sb = sb("ws_sb", [P, NX])
        bs_bc = sb("bs_bc", [P, NX])
        ident = sb("ident", [P, P])
        mean_w = sb("mean_w", [P, P])
        sel0 = sb("sel0", [3 * NX, P], BF16)
        ones_bf = sb("ones_bf", [P, P], BF16)
        earlier = sb("earlier", [P, P], BF16)
        keep = sb("keep", [P, 2, P])
        restart = sb("restart", [P, 2 * HTOK], BF16)
        pow_half = sb("pow_half", [P, 4])
        rev = sb("rev", [P, NX])
        base = sb("base", [P, NX])
        steps = sb("steps", [P, NX])
        before = sb("before", [P, NX, NX])
        tile_no = sb("tile_no", [P, TILES])
        pidx = sb("pidx", [P, 1], I32)
        pidx8 = sb("pidx8", [P, 1], I32)
        pmod = sb("pmod", [P, 1], I32)
        pmod_f = sb("pmod_f", [P, 1])
        tok_f = sb("tok_f", [P, 2])
        token = sb("token", [P, NT])
        part = sb("part", [P, 4])
        zero_row = sb("zero_row", [P, ROW])
        hraw = sb("hraw", [P, NU, D])
        stats = sb("stats", [P, NU, 6])
        mv = sb("mv", [P, NU, 2])
        tiny = sb("tiny", [P, NU, 2])
        scale = sb("scale", [P, NU])
        xn = sb("xn", [P, NU, D])
        xnT = sb("xnT", [P, HTOK])
        gl = sb("gl", [P, HP, HTOK])
        cum = sb("cum", [P, HP, HTOK])
        ginv = sb("ginv", [P, HP, HTOK])
        kraw = sb("kraw", [P, 2, HTOK])
        qraw = sb("qraw", [P, 2, HTOK])
        ks = sb("ks", [P, 2, HP, HTOK])
        qs = sb("qs", [P, 2, HTOK])
        vv = sb("vv", [P, 2, NU, INNER])
        att = sb("att", [P, 4, 2, HTOK])
        aoT = sb("aoT", [P, HP, HTOK])
        rows = sb("rows", [P, NT, ROW])
        h1T = xnT
        wc_sb = sb("wc_sb", [P, NX])
        lg = sb("lg", [P, NU, NX])
        mx = sb("mx", [P, NU])
        cand = sb("cand", [P, NU, NX])
        cm = sb("cm", [P, NT])
        ex = sb("ex", [P, NU, NX])
        esum = sb("esum", [P, NU])
        ohb = sb("ohb", [P, NT, NX], BF16)
        rank = sb("rank", [P, NT, NX])
        cnt = sb("cnt", [P, NX])
        cmp = sb("cmp", [P, NX, NX])
        ntile = sb("ntile", [P, NX])
        first = sb("first", [P, NX])
        last = sb("last", [P, NX])
        slot_f = sb("slot_f", [P, NT])
        slot_i = sb("slot_i", [P, NT], I32)
        owner_c = sb("owner_c", [P, TILES, NX])
        owner_f = sb("owner_f", [P, TILES])
        owner_i = sb("owner_i", [P, TILES], I32)
        bias_f = aoT[0:3 * NX, :, :].rearrange("p a b -> p (a b)")[:, 0:NBIAS]
        bias_r = att[0:3 * NX, 0:2, :, :].rearrange("p a b c -> p (a b c)")[:, 0:NBIAS]
        bias_p = [b[0:3 * NX, 0:2, :].rearrange("p a b -> p (a b)").bitcast(BF16)[:, 0:NBIAS] for b in (gl, cum, ginv)]
        bias_b = sb("bias_b", [3 * NX, NBIAS], BF16)
        pick = sb("pick", [3 * NX, TILES, P], BF16)
        srow = ks[:, :, :, :].rearrange("p a b c -> p (a b c)")[:, 0:TILES * ROW].rearrange("p (t r) -> p t r", r=ROW)
        sx = gl[:, 0, :].rearrange("p (a b) -> p a b", a=4)
        sxT = gl[:, 1, :].rearrange("p (a b) -> p a b", a=4)
        hid = cum[:, 0:2, :]
        hidT = cum[:, 2:4, :]
        fin = ginv[:, 0, :].rearrange("p (a b) -> p a b", a=4)
        fin0 = ginv[:, 1, :].rearrange("p (a b) -> p a b", a=4)
        dest_f = sb("dest_f", [P, TILES])
        dest = sb("dest", [P, TILES], I32)

        bank = [ctx.enter_context(nc.psum_tensor(f"bank{i}", [P, 512], F32)) for i in range(8)]
        h_rows = nc.dram_tensor("h_rows", [2, B, EH * D], F32, kind="Internal").ap()
        sorted_rows = nc.dram_tensor("sorted_rows", [TILES * P, ROW], F32, kind="Internal").ap()

        slot_in = [sem(f"slot_in{i}") for i in range(NSLOT)]
        x_in = sem("x_in")
        tokb_in = sem("tokb_in")
        small_in = sem("small_in")
        bias_in = sem("bias_in")
        bias_done = sem("bias_done")
        wa_in = sem("wa_in")
        wv_in = sem("wv_in")
        wqk_in = sem("wqk_in")
        wout_in = sem("wout_in")
        w1_in = sem("w1_in")
        w2_in = sem("w2_in")
        h_out = sem("h_out")
        res_in = sem("res_in")
        zeroed = sem("zeroed")
        spread = sem("spread")
        srow_in = [sem(f"srow_in{i}") for i in range(4)]
        stored = [sem(f"stored{i}") for i in range(4)]
        const_pool = sem("const_pool")
        pool_step = sem("pool_step")
        dve_step = sem("dve_step")
        const_dve = sem("const_dve")
        masked = sem("masked")
        used = sem("used")
        raw_done = sem("raw_done")
        var_done = sem("var_done")
        scale_done = sem("scale_done")
        xn_done = sem("xn_done")
        xnT_ps = sem("xnT_ps")
        xnT_done = sem("xnT_done")
        gate_ps = sem("gate_ps")
        gate_exp = sem("gate_exp")
        gate_clip = sem("gate_clip")
        gate_ln = sem("gate_ln")
        gate_cum = sem("gate_cum")
        gate_cap = sem("gate_cap")
        gate_a = sem("gate_a")
        gate_inv = sem("gate_inv")
        v_ps = sem("v_ps")
        v_done = sem("v_done")
        k_ps = sem("k_ps")
        k_raw = sem("k_raw")
        q_raw = sem("q_raw")
        k_done = sem("k_done")
        q_ps = sem("q_ps")
        q_done = sem("q_done")
        sim_ps = sem("sim_ps")
        att_done = sem("att_done")
        ao_ps = sem("ao_ps")
        ao_done = sem("ao_done")
        y_ps = sem("y_ps")
        h1_done = sem("h1_done")
        var2_done = sem("var2_done")
        scale2_done = sem("scale2_done")
        h1T_ps = sem("h1T_ps")
        h1T_done = sem("h1T_done")
        colmean_ps = sem("colmean_ps")
        wc_done = sem("wc_done")
        lg_ps = sem("lg_ps")
        lm_done = sem("lm_done")
        ex_done = sem("ex_done")
        oh_done = sem("oh_done")
        rank_ps = sem("rank_ps")
        rank_done = sem("rank_done")
        cnt_ps = sem("cnt_ps")
        slot_done = sem("slot_done")
        owner_done = sem("owner_done")
        pick_done = sem("pick_done")
        sx_done = sem("sx_done")
        sxT_ps = sem("sxT_ps")
        sxT_done = sem("sxT_done")
        hid_ps = sem("hid_ps")
        hid_done = sem("hid_done")
        hidT_ps = sem("hidT_ps")
        hidT_done = sem("hidT_done")
        ffn_ps = sem("ffn_ps")
        fin0_done = sem("fin0_done")
        fin_done = sem("fin_done")
        dest_done = sem("dest_done")

        block = ctx.enter_context(nc.Block())

        def rows_of(c):
            ts = (GT - 1, GT) if c == 0 else range(TC * (c - 1), TC * c)
            return [(t, P if t < GT else GREM) for t in ts]

        def slot_in_count(n):
            total = 0
            for m in range(n % NSLOT, n + 1, NSLOT):
                h, c = divmod(m, NCH)
                dmas = 2 if c == 0 else 1
                total += 16 * dmas * (2 if h == 0 else 1)
            return total

        def masked_count(n):
            return sum(3 if m % NCH == 0 else 2 for m in range(n + 1))

        def chunk_view(n):
            return ring[:, n % NSLOT, :].rearrange("p (e t d) -> p e t d", e=EH, t=TC)

        w_main = weight[:, 0:GT * P, :].rearrange("e (p t) d -> p e t d", t=GT)
        w_rest = weight[:, GT * P:G, :].rearrange("e p d -> p e d")
        m_main = mask[0:GT * P, :].rearrange("(p t) d -> p t d", t=GT)
        m_rest = mask[GT * P:G, :]
        x_main = x_t[0:GT * P, :].rearrange("(p t) b -> p t b", t=GT)
        x_rest = x_t[GT * P:G, :]

        class Ahead:

            def __init__(self):
                self.next = NCH

            def after(self, stage, half):
                n0 = self.next
                if half == 0:
                    count = AHEAD[stage] if stage != "route" else 2 * NCH - n0
                    self.next = min(2 * NCH, n0 + count)
                return range(n0, self.next)

        def sim_group(half, hp, key_half):
            return hp if half == 0 else HP + 2 * hp + key_half

        def group_reader(n):
            return n + 1 if n < HP else HP + (n - HP) // 2 + 1

        @block.sync
        def _(sp):
            def load_chunk(n):
                half, c = divmod(n, NCH)
                s = slot_in[n % NSLOT]
                if n >= NSLOT:
                    sp.wait_ge(used, n - NSLOT + 1)
                ts = [t for t, k in rows_of(c) if k == P]
                t0, t1 = ts[0], ts[-1] + 1
                v = chunk_view(n)
                if half == 0:
                    sp.dma_start(maskt[:, t0:t1, :], m_main[:, t0:t1, :]).then_inc(s, 16)
                sp.dma_start(v[:, :, 0:t1 - t0, :], w_main[:, half * EH:(half + 1) * EH, t0:t1, :]).then_inc(s, 16)
                if c == 0:
                    if half == 0:
                        sp.dma_start(maskt[0:GREM, GT, :], m_rest).then_inc(s, 16)
                    sp.dma_start(v[0:GREM, :, 1, :], w_rest[:, half * EH:(half + 1) * EH, :]).then_inc(s, 16)

            for n in range(2 * NCH):
                load_chunk(n)
                if n == 0:
                    sp.dma_start(xT[0:GREM, GT, :], x_rest).then_inc(x_in, 16)
                    sp.dma_start(xT[:, 0:GT, :], x_main).then_inc(x_in, 16)
                if n == NCH - 1:
                    sp.dma_start(wa_sb[:], w_a).then_inc(wa_in, 16)
                    sp.dma_start(wqkv_sb[:, 2 * INNER:3 * INNER], w_qkv[:, 2 * INNER:3 * INNER]).then_inc(wv_in, 16)
                if n == NCH:
                    sp.dma_start(wqkv_sb[:, 0:2 * INNER], w_qkv[:, 0:2 * INNER]).then_inc(wqk_in, 16)
                    sp.dma_start(wout_sb[:], w_out.rearrange("(c p) d -> p c d", p=P)).then_inc(wout_in, 16)
                if n == NCH + 8:
                    sp.wait_ge(const_pool, NCONST)
                    sp.dma_start(sorted_rows.rearrange("(t p) r -> p t r", p=P),
                                 zero_row[:].rearrange("p (a r) -> p a r", a=1).broadcast_to([P, TILES, ROW]))\
                        .then_inc(zeroed, 16)
            sp.wait_ge(used, 2 * NCH)
            sp.dma_start(w1_sb.rearrange("p (e f) -> p e f", e=NX), w1.rearrange("e d f -> d e f")).then_inc(w1_in, 16)
            sp.dma_start(w2_sb.rearrange("p (e c d) -> p e c d", e=NX, c=FC),
                         w2.rearrange("e (c p) d -> p e c d", p=P)).then_inc(w2_in, 16)
            sp.wait_ge(spread, 16 * NT)
            sp.wait_ge(ao_ps, 2 * HP)
            for j in range(TILES):
                if j >= 4:
                    sp.wait_ge(srow_in[j % 4], 16 * (j // 4))
                sp.dma_start(srow[:, j, :], sorted_rows[j * P:(j + 1) * P, :]).then_inc(srow_in[j % 4], 16)

        @block.gpsimd
        def _(pool):
            count = [0]

            def link(ins):
                count[0] += 1
                ins.then_inc(pool_step, 1)
                pool.wait_ge(pool_step, count[0])

            link(nc.gpsimd.memset(ident[:], 0.0))
            nc.gpsimd.affine_select(out=ident[:], in_=ident[:], compare_op=ALU.not_equal, fill=1.0, base=0,
                                    pattern=[[-1, P]], channel_multiplier=1).then_inc(const_pool, 1)
            nc.gpsimd.memset(ones_bf[:], 1.0).then_inc(const_pool, 1)
            nc.gpsimd.memset(pow_half[:], -0.5).then_inc(const_pool, 1)
            link(nc.gpsimd.memset(earlier[:], 1.0))
            nc.gpsimd.affine_select(out=earlier[:], in_=earlier[:], compare_op=ALU.is_gt, fill=0.0, base=0,
                                    pattern=[[1, P]], channel_multiplier=-1).then_inc(const_pool, 1)
            link(nc.gpsimd.memset(keep[:], SCALE))
            for s in range(2):
                v = keep[:, s, :].rearrange("p (b e) -> p b e", e=EH)
                link(nc.gpsimd.affine_select(out=v, in_=v, compare_op=ALU.is_ge, fill=0.0, base=0,
                                             pattern=[[-EH, UB], [0, EH]], channel_multiplier=1))
                link(nc.gpsimd.affine_select(out=v, in_=v, compare_op=ALU.is_ge, fill=0.0, base=EH - 1,
                                             pattern=[[EH, UB], [0, EH]], channel_multiplier=-1))
            nc.gpsimd.affine_select(out=keep[:, 0, :], in_=keep[:, 0, :], compare_op=ALU.is_ge, fill=0.0, base=0,
                                    pattern=[[1, P]], channel_multiplier=-1).then_inc(const_pool, 1)
            link(nc.gpsimd.memset(restart[:], 1.0))
            nc.gpsimd.memset(restart[:].rearrange("p (b e) -> p b e", e=EH)[:, :, 0:1], 0.0).then_inc(const_pool, 1)
            small = dict(allow_small_or_imprecise_dtypes=True)
            nc.gpsimd.iota(rev[:], [[-1, NX]], base=NX, channel_multiplier=0, **small).then_inc(const_pool, 1)
            nc.gpsimd.iota(steps[:], [[P, NX]], base=0, channel_multiplier=0, **small).then_inc(const_pool, 1)
            nc.gpsimd.iota(tile_no[:], [[1, TILES]], base=0, channel_multiplier=0, **small).then_inc(const_pool, 1)
            nc.gpsimd.iota(pidx[:], [[0, 1]], base=0, channel_multiplier=1).then_inc(const_pool, 1)
            link(nc.gpsimd.memset(before[:], 1.0))
            nc.gpsimd.affine_select(out=before[:], in_=before[:], compare_op=ALU.is_gt, fill=0.0, base=0,
                                    pattern=[[1, NX], [-1, NX]], channel_multiplier=0).then_inc(const_pool, 1)
            link(nc.gpsimd.memset(part[:], 1.0))
            link(nc.gpsimd.affine_select(out=part[:, 0:3], in_=part[:, 0:3], compare_op=ALU.is_ge, fill=0.0, base=0,
                                         pattern=[[-NX, 3]], channel_multiplier=1))
            nc.gpsimd.affine_select(out=part[:, 0:3], in_=part[:, 0:3], compare_op=ALU.is_ge, fill=0.0, base=NX - 1,
                                    pattern=[[NX, 3]], channel_multiplier=-1).then_inc(const_pool, 1)
            nc.gpsimd.memset(zero_row[:], 0.0).then_inc(const_pool, 1)
            nc.gpsimd.memset(mean_w[:], 1.0 / D).then_inc(const_pool, 1)

            for half in range(2):
                pool.wait_ge(var_done, half + 1)
                nc.gpsimd.tensor_tensor(scale[:], tiny[:, :, 1], pow_half[:], ALU.pow).then_inc(scale_done, 1)
                pool.wait_ge(raw_done, half + 1)
                for s in range(2):
                    pool.dma_start(h_rows[half, :, s * NU * D:(s + 1) * NU * D],
                                   hraw[s * B:(s + 1) * B, :, :].rearrange("p u d -> p (u d)")).then_inc(h_out, 16)
                pool.wait_ge(h_out, 32 * (half + 1))
                pool.dma_start(rows[:, half * NU:(half + 1) * NU, 0:D],
                               h_rows[half].rearrange("(u c) (e d) -> (c e) u d", c=UB, e=EH)).then_inc(res_in, 16)
                pool.wait_ge(var2_done, half + 1)
                nc.gpsimd.tensor_tensor(scale[:], tiny[:, :, 1], pow_half[:], ALU.pow).then_inc(scale2_done, 1)
            pool.wait_ge(slot_done, 1)
            pool.wait_ge(zeroed, 16)
            for t in range(NT):
                pool.indirect_dma_start(out=sorted_rows, out_offset=bass.IndirectOffsetOnAxis(ap=slot_i[:, t:t + 1], axis=0),
                                        in_=rows[:, t, :], in_offset=None).then_inc(spread, 16)
            pool.wait_ge(dest_done, 1)
            out_rows = out.rearrange("b e d -> (b e) d")
            for j in range(TILES):
                pool.wait_ge(fin_done, j + 1)
                pool.indirect_dma_start(out=out_rows, out_offset=bass.IndirectOffsetOnAxis(ap=dest[:, j:j + 1], axis=0),
                                        in_=fin[:, j % 4, :], in_offset=None,
                                        bounds_check=NTOK - 1, oob_is_err=False).then_inc(stored[j % 4], 16)
            for k in range(4):
                pool.wait_ge(stored[k], 16 * len(range(k, TILES, 4)))

        @block.scalar
        def _(act):
            for half in range(2):
                for s in range(2):
                    e0 = half * EH + s * NU
                    src = tok_bias[e0:e0 + NU, :].rearrange("(a e) d -> a (e d)", a=1)
                    act.dma_start(tokb_bc[s * B:(s + 1) * B, half, :], src.broadcast_to([B, NU * D])).then_inc(tokb_in, 16)
            for dst, src in ((gamma_sb[:], gamma), (bq_sb[:], bq), (bk_sb[:], bk), (ba_sb[:], ba), (ws_sb[:], w_s),
                             (bs_bc[:], b_s.broadcast_to([P, NX]))):
                act.dma_start(dst, src).then_inc(small_in, 16)
            for i in range(3):
                act.dma_start(bias_f[i * NX:(i + 1) * NX, B1], b1).then_inc(bias_in, 16)
                act.dma_start(bias_f[i * NX:(i + 1) * NX, B2], b2).then_inc(bias_in, 16)
            act.dma_start(bias_f[:, BV], b_v.broadcast_to([3 * NX, INNER])).then_inc(bias_in, 16)
            act.dma_start(bias_f[:, BO], b_out.broadcast_to([3 * NX, D])).then_inc(bias_in, 16)
            act.preload_act_table_set("natural_log_exp_and_others")
            act.wait_ge(small_in, 16 * 6)
            act.wait_ge(const_dve, 1)
            for half in range(2):
                act.wait_ge(xnT_ps, half + 1)
                if half:
                    act.wait_ge(lg_ps, half)
                nc.scalar.activation(xnT[:].rearrange("p (b s e) -> p e s b", s=2, e=NU),
                                     bank[1][:].rearrange("p (e s b) -> p e s b", s=2, b=B),
                                     ACT.Copy, scale=gamma_sb[:, 0:1]).then_inc(xnT_done, 1)

                def gate(g):
                    act.wait_ge(gate_cum, 2 * half + g + 1)
                    nc.scalar.activation(gl[:, 2 * g:2 * g + 2, :], cum[:, 2 * g:2 * g + 2, :], ACT.Exp, scale=-1.0)\
                        .then_inc(gate_a, 1)
                    act.wait_ge(gate_cap, 2 * half + g + 1)
                    nc.scalar.activation(ginv[:, 2 * g:2 * g + 2, :], ginv[:, 2 * g:2 * g + 2, :], ACT.Exp)\
                        .then_inc(gate_inv, 1)

                def gate_log(g):
                    act.wait_ge(gate_clip, 2 * half + g + 1)
                    nc.scalar.activation(gl[:, 2 * g:2 * g + 2, :], gl[:, 2 * g:2 * g + 2, :], ACT.Ln)\
                        .then_inc(gate_ln, 1)

                def values(u):
                    act.wait_ge(v_ps, half * NU + u + 1)
                    nc.scalar.activation(vv[:, half, u, :], bank[2 + u % 2][:], ACT.Copy).then_inc(v_done, 1)

                def key_query(hp):
                    i = half * HP + hp
                    act.wait_ge(k_ps, i + 1)
                    if i >= 2:
                        act.wait_ge(k_done, i - 1)
                    nc.scalar.activation(kraw[:, i % 2, :], bank[2][:], ACT.Identity, bias=bk_sb[:, hp:hp + 1])\
                        .then_inc(k_raw, 1)
                    act.wait_ge(q_ps, i + 1)
                    if i >= 2:
                        act.wait_ge(q_done, i - 1)
                    nc.scalar.activation(qraw[:, i % 2, :], bank[3][:], ACT.Identity, bias=bq_sb[:, hp:hp + 1])\
                        .then_inc(q_raw, 1)

                for hp in range(HP):
                    act.wait_ge(gate_ps, half * HP + hp + 1)
                    if half and hp == 0:
                        act.wait_ge(q_done, HP)
                    if half == 0 and hp == 0:
                        act.wait_ge(bias_done, 1)
                    nc.scalar.activation(gl[:, hp, :], bank[4 + hp][:], ACT.Exp, scale=-1.0,
                                         bias=nba_sb[:, hp:hp + 1]).then_inc(gate_exp, 1)
                values(0)
                values(1)
                gate_log(0)
                gate_log(1)
                values(2)
                values(3)
                key_query(0)
                gate(0)
                key_query(1)
                gate(1)
                for hp in range(HP):
                    if hp + 2 < HP:
                        key_query(hp + 2)
                    i = half * HP + hp
                    act.wait_ge(ao_ps, i + 1)
                    if half and hp == 0:
                        act.wait_ge(y_ps, half)
                    nc.scalar.activation(aoT[:, hp, :], bank[1][:], ACT.Copy).then_inc(ao_done, 1)
                act.wait_ge(h1T_ps, half + 1)
                nc.scalar.activation(h1T[:], bank[1][:], ACT.Copy).then_inc(h1T_done, 1)
                act.wait_ge(lm_done, half + 1)
                nc.scalar.activation(ex[:], lg[:], ACT.Exp).then_inc(ex_done, 1)
            def take_xT(j):
                act.wait_ge(sxT_ps, j + 1)
                if j >= 4:
                    act.wait_ge(hid_ps, j - 3)
                nc.scalar.activation(sxT[:, j % 4, :], bank[j % 2][:, 0:P], ACT.Copy).then_inc(sxT_done, 1)

            take_xT(0)
            take_xT(1)
            for j in range(TILES):
                act.wait_ge(hid_ps, j + 1)
                if j >= 2:
                    act.wait_ge(hidT_ps, j - 1)
                nc.scalar.activation(hid[:, j % 2, :], bank[2 + j % 2][:], ACT.Gelu).then_inc(hid_done, 1)
                if j + 2 < TILES:
                    take_xT(j + 2)

        @block.vector
        def _(dve):
            count = [0]
            ahead = Ahead()

            def link(ins):
                count[0] += 1
                ins.then_inc(dve_step, 1)
                dve.wait_ge(dve_step, count[0])

            def mask_chunk(n):
                half, c = divmod(n, NCH)
                dve.wait_ge(slot_in[n % NSLOT], slot_in_count(n))
                v = chunk_view(n)
                ts = [t for t, k in rows_of(c) if k == P]
                t0, w = ts[0], len(ts)
                for s in range(2):
                    part_v = v[:, s * NU:(s + 1) * NU, 0:w, :]
                    m = maskt[:, t0:t0 + w, :].rearrange("p (a t) d -> p a t d", a=1).broadcast_to([P, NU, w, D])
                    nc.vector.tensor_tensor(part_v, part_v, m, ALU.mult).then_inc(masked, 1)
                if c == 0:
                    part_v = v[0:GREM, :, 1, :]
                    m = maskt[0:GREM, GT:GT + 1, :].broadcast_to([GREM, EH, D])
                    nc.vector.tensor_tensor(part_v, part_v, m, ALU.mult).then_inc(masked, 1)

            def moments(src, s6):
                for u in range(NU):
                    ins = nc.vector.bn_stats(s6[:, u, :], src(u))
                    if u == NU - 1:
                        link(ins)
                    else:
                        ins.then_inc(dve_step, 1)
                        count[0] += 1
                for u in range(NU):
                    ins = nc.vector.bn_aggr(mv[:, u, :], s6[:, u, :])
                    if u == NU - 1:
                        link(ins)
                    else:
                        ins.then_inc(dve_step, 1)
                        count[0] += 1

            def constants():
                dve.wait_ge(const_pool, NCONST)
                link(nc.vector.tensor_single_scalar(pidx8[:], pidx[:], -EH, ALU.bitwise_and))
                link(nc.vector.tensor_single_scalar(pmod[:], pidx[:], NX - 1, ALU.bitwise_and))
                link(nc.vector.tensor_copy(pmod_f[:], pmod[:]))
                link(nc.vector.tensor_copy(tok_f[:, 0:1], pidx[:]))
                link(nc.vector.tensor_copy(tok_f[:, 1:2], pidx8[:]))
                link(nc.vector.tensor_tensor(tok_f[:, 0:1], tok_f[:, 0:1], tok_f[:, 1:2], ALU.add))
                for t in range(NT):
                    half, u = divmod(t, NU)
                    link(nc.vector.tensor_scalar_add(rows[:, t, D + 3:D + 4], tok_f[:, 0:1],
                                                     float(u * UB * E + half * EH) - NO_TOKEN))
                dve.wait_ge(small_in, 16 * 6)
                nc.vector.tensor_scalar_mul(nba_sb[:], ba_sb[:], -1.0).then_inc(const_dve, 1)
                nc.vector.tensor_scalar(sel0[:], ones_bf[0:3 * NX, :], 0.0, pmod_f[0:3 * NX, 0:1], ALU.mult,
                                        ALU.is_equal).then_inc(const_dve, 1)

            def bias_parts(step):
                if step == 0:
                    dve.wait_ge(bias_in, 16 * 8)
                    link(nc.vector.tensor_copy(bias_p[0], bias_f))
                    link(nc.vector.tensor_tensor(bias_r, bias_f, bias_p[0], ALU.subtract))
                elif step == 1:
                    link(nc.vector.tensor_copy(bias_p[1], bias_r))
                    link(nc.vector.tensor_tensor(bias_p[2], bias_r, bias_p[1], ALU.subtract))
                elif step == 2:
                    link(nc.vector.tensor_scalar(bias_r, bias_p[0], part[0:3 * NX, 0:1], None, ALU.mult))
                    link(nc.vector.scalar_tensor_tensor(bias_r, bias_p[1], part[0:3 * NX, 1:2], bias_r,
                                                        ALU.mult, ALU.add))
                else:
                    nc.vector.scalar_tensor_tensor(bias_b[:], bias_p[2], part[0:3 * NX, 2:3], bias_r,
                                                   ALU.mult, ALU.add).then_inc(bias_done, 1)

            for n in range(NCH):
                if n == 3:
                    constants()
                if 6 <= n < 10:
                    bias_parts(n - 6)
                if n == 11:
                    dve.wait_ge(colmean_ps, 1)
                    nc.vector.tensor_tensor(wc_sb[:], ws_sb[:], bank[3][:, 0:NX], ALU.subtract).then_inc(wc_done, 1)
                mask_chunk(n)
            dve.wait_ge(tokb_in, 16 * 4)
            for n in range(NCH, NCH + LEAD):
                mask_chunk(n)

            for half in range(2):
                def after(stage):
                    for n in ahead.after(stage, half):
                        if n + LEAD < 2 * NCH:
                            mask_chunk(n + LEAD)

                dve.wait_ge(used, NCH * (half + 1))
                if half:
                    dve.wait_ge(h_out, 32)
                nc.vector.tensor_tensor(hraw[:].rearrange("p u d -> p (u d)"), bank[0][:], tokb_bc[:, half, :],
                                        ALU.add).then_inc(raw_done, 1)
                dve.wait_ge(raw_done, half + 1)
                moments(lambda u: hraw[:, u, :], stats)
                floor = NORM_FLOOR ** 2 / D
                link(nc.vector.tensor_scalar(tiny[:, :, 0], mv[:, :, 1], LN_EPS, floor, ALU.add, ALU.mult))
                nc.vector.tensor_tensor(tiny[:, :, 1], mv[:, :, 1], tiny[:, :, 0], ALU.max).then_inc(var_done, 1)
                dve.wait_ge(scale_done, half + 1)
                for u in range(NU):
                    nc.vector.tensor_scalar(xn[:, u, :], hraw[:, u, :], mv[:, u, 0:1], scale[:, u:u + 1],
                                            ALU.subtract, ALU.mult).then_inc(xn_done, 1)
                after("norm")
                for g in range(2):
                    gs = gl[:, 2 * g:2 * g + 2, :]
                    dve.wait_ge(gate_exp, half * HP + 2 * g + 2)
                    nc.vector.tensor_scalar(gs, gs, 1.0, 1.0 / A_FLOOR, ALU.add, ALU.min).then_inc(gate_clip, 1)
                after("gates")
                for g in range(2):
                    gs = gl[:, 2 * g:2 * g + 2, :]
                    cs = cum[:, 2 * g:2 * g + 2, :]
                    dve.wait_ge(gate_ln, 2 * half + g + 1)
                    if half:
                        gv = gs.rearrange("p c (b e) -> p c b e", e=EH)[:, :, :, 0]
                        cv = cs.rearrange("p c (b e) -> p c b e", e=EH)[:, :, :, EH - 1]
                        dve.wait_ge(gate_cum, 2)
                        link(nc.vector.tensor_tensor(gv, gv, cv, ALU.add))
                        dve.wait_ge(gate_a, 2)
                    nc.vector.tensor_tensor_scan(cs.rearrange("p c t -> p (c t)"), restart[:],
                                                 gs.rearrange("p c t -> p (c t)"), 0.0, ALU.mult, ALU.add)\
                        .then_inc(gate_cum, 1)
                    dve.wait_ge(gate_cum, 2 * half + g + 1)
                    if half:
                        dve.wait_ge(k_done, HP)
                    nc.vector.tensor_scalar_min(ginv[:, 2 * g:2 * g + 2, :], cs, 40.0).then_inc(gate_cap, 1)
                after("values")

                def scaled_key_query(hp):
                    i = half * HP + hp
                    dve.wait_ge(k_raw, i + 1)
                    dve.wait_ge(gate_inv, 2 * half + hp // 2 + 1)
                    nc.vector.scalar_tensor_tensor(ks[:, half, hp, :], ginv[:, hp, :], 1.0 / INV_FLOOR, kraw[:, i % 2, :],
                                                   ALU.min, ALU.mult).then_inc(k_done, 1)
                    dve.wait_ge(q_raw, i + 1)
                    if i >= 2:
                        dve.wait_ge(sim_ps, sim_group((i - 2) // HP, (i - 2) % HP, (i - 2) // HP) + 1)
                    nc.vector.tensor_tensor(qs[:, i % 2, :], qraw[:, i % 2, :], gl[:, hp, :], ALU.mult).then_inc(q_done, 1)

                def mask_scores(hp):
                    for key_half in range(half + 1):
                        n = sim_group(half, hp, key_half)
                        dve.wait_ge(sim_ps, n + 1)
                        if n >= 4:
                            dve.wait_ge(ao_ps, group_reader(n - 4))
                        m = keep[:, int(key_half < half), :].rearrange("p (a i) -> p a i", a=1).broadcast_to([P, NU, P])
                        for odd in range(2):
                            nc.vector.tensor_tensor(att[:, n % 4, odd, :].rearrange("p (u i) -> p u i", u=NU),
                                                    bank[4 + 2 * (n % 2) + odd][:].rearrange("p (u i) -> p u i", u=NU),
                                                    m, ALU.mult).then_inc(att_done, 1)

                scaled_key_query(0)
                scaled_key_query(1)
                after("first")
                for hp in range(HP):
                    mask_scores(hp)
                    if hp + 2 < HP:
                        scaled_key_query(hp + 2)
                    after(f"pair{hp}")

                tiles = slice(half * NU, (half + 1) * NU)
                h1 = rows[:, tiles, 0:D]
                dve.wait_ge(res_in, 16 * (half + 1))
                dve.wait_ge(y_ps, half + 1)
                nc.vector.tensor_tensor(h1, h1, bank[2][:].rearrange("p (u d) -> p u d", u=NU), ALU.add)\
                    .then_inc(h1_done, 1)
                dve.wait_ge(h1_done, half + 1)
                after("project")
                moments(lambda u: rows[:, half * NU + u, 0:D], stats)
                nc.vector.tensor_scalar_add(tiny[:, :, 1], mv[:, :, 1], LN_EPS).then_inc(var2_done, 1)
                link(nc.vector.tensor_copy(rows[:, tiles, D], mv[:, :, 0]))
                dve.wait_ge(scale2_done, half + 1)
                link(nc.vector.tensor_copy(rows[:, tiles, D + 1], scale[:]))

                def over_x(ap):
                    return ap.rearrange("p (u a) -> p u a", a=1).broadcast_to([P, NU, NX])

                def over_u(ap):
                    return ap.rearrange("p (a x) -> p a x", a=1).broadcast_to([P, NU, NX])

                dve.wait_ge(lg_ps, half + 1)
                if half:
                    dve.wait_ge(ex_done, half)
                link(nc.vector.tensor_tensor(lg[:], bank[3][:, 0:NU * NX].rearrange("p (u x) -> p u x", u=NU),
                                             over_x(scale[:]), ALU.mult))
                link(nc.vector.tensor_tensor(lg[:], lg[:], over_u(bs_bc[:]), ALU.add))
                link(nc.vector.tensor_reduce(mx[:], lg[:], AX.X, ALU.max))
                nc.vector.tensor_tensor(lg[:], lg[:], over_x(mx[:]), ALU.subtract).then_inc(lm_done, 1)
                dve.wait_ge(lm_done, half + 1)
                link(nc.vector.scalar_tensor_tensor(cand[:], lg[:], 0.0, over_u(rev[:]), ALU.is_ge, ALU.mult))
                link(nc.vector.tensor_reduce(cm[:, tiles], cand[:], AX.X, ALU.max))
                nc.vector.tensor_tensor(ohb[:, tiles, :], cand[:], over_x(cm[:, tiles]), ALU.is_equal).then_inc(oh_done, 1)
                dve.wait_ge(ex_done, half + 1)
                link(nc.vector.tensor_reduce(esum[:], ex[:], AX.X, ALU.add))
                link(nc.vector.reciprocal(rows[:, tiles, D + 2], esum[:]))
                after("route")

            def over_t(ap):
                return ap.rearrange("p (a x) -> p a x", a=1).broadcast_to([P, NT, NX])

            dve.wait_ge(rank_ps, 1)
            link(nc.vector.tensor_copy(cnt[:], bank[2][:, 0:NX]))
            link(nc.vector.tensor_tensor(cmp[:], cnt[:].rearrange("p (x a) -> p x a", a=1).broadcast_to([P, NX, NX]),
                                         steps[:].rearrange("p (a k) -> p a k", a=1).broadcast_to([P, NX, NX]), ALU.is_gt))
            link(nc.vector.tensor_reduce(ntile[:], cmp[:], AX.X, ALU.add))
            link(nc.vector.tensor_tensor(cmp[:], before[:],
                                         ntile[:].rearrange("p (a k) -> p a k", a=1).broadcast_to([P, NX, NX]), ALU.mult))
            link(nc.vector.tensor_reduce(first[:], cmp[:], AX.X, ALU.add))
            link(nc.vector.tensor_scalar_mul(base[:], first[:], float(P)))
            link(nc.vector.tensor_tensor(rank[:], bank[3][:, 0:NT * NX].rearrange("p (t x) -> p t x", t=NT),
                                         over_t(base[:]), ALU.add))
            link(nc.vector.tensor_tensor(rank[:], rank[:], ohb[:], ALU.mult))
            link(nc.vector.tensor_reduce(slot_f[:], rank[:], AX.X, ALU.add))
            nc.vector.tensor_copy(slot_i[:], slot_f[:]).then_inc(slot_done, 1)
            link(nc.vector.tensor_tensor(last[:], first[:], ntile[:], ALU.add))
            link(nc.vector.tensor_tensor(owner_c[:], tile_no[:].rearrange("p (t a) -> p t a", a=1).broadcast_to([P, TILES, NX]),
                                         last[:].rearrange("p (a x) -> p a x", a=1).broadcast_to([P, TILES, NX]), ALU.is_ge))
            link(nc.vector.tensor_reduce(owner_f[:], owner_c[:], AX.X, ALU.add))
            link(nc.vector.tensor_scalar_min(owner_f[:], owner_f[:], float(NX - 1)))
            nc.vector.tensor_copy(owner_i[:], owner_f[:]).then_inc(owner_done, 1)
            nc.vector.tensor_scalar(pick[:], owner_f[0:3 * NX, :].rearrange("p (t a) -> p t a", a=1)
                                    .broadcast_to([3 * NX, TILES, P]), pmod_f[0:3 * NX, 0:1], None, ALU.is_equal)\
                .then_inc(pick_done, 1)

            def normalise(j):
                dve.wait_ge(srow_in[j % 4], 16 * (j // 4 + 1))
                if j >= 4:
                    dve.wait_ge(sxT_ps, j - 3)
                nc.vector.tensor_scalar(sx[:, j % 4, :], srow[:, j, 0:D], srow[:, j, D:D + 1], srow[:, j, D + 1:D + 2],
                                        ALU.subtract, ALU.mult).then_inc(sx_done, 1)

            def take_hidT(j):
                dve.wait_ge(hidT_ps, j + 1)
                if j >= 2:
                    dve.wait_ge(ffn_ps, j - 1)
                nc.vector.tensor_copy(hidT[:, j % 2, :], bank[4 + j % 2][:]).then_inc(hidT_done, 1)

            def finish(j):
                dve.wait_ge(ffn_ps, j + 1)
                if j >= 4:
                    dve.wait_ge(stored[j % 4], 16 * (j // 4))
                nc.vector.scalar_tensor_tensor(fin[:, j % 4, :], bank[6 + j % 2][:, 0:D], srow[:, j, D + 2:D + 3],
                                               srow[:, j, 0:D], ALU.mult, ALU.add).then_inc(fin_done, 1)

            normalise(0)
            normalise(1)
            for j in range(TILES + 2):
                if j + 2 < TILES:
                    normalise(j + 2)
                if j == 1:
                    for k in range(4):
                        dve.wait_ge(srow_in[k], 16 * len(range(k, TILES, 4)))
                    link(nc.vector.tensor_scalar_add(dest_f[:], srow[:, :, D + 3], NO_TOKEN))
                    nc.vector.tensor_copy(dest[:], dest_f[:]).then_inc(dest_done, 1)
                if 1 <= j < TILES + 1:
                    take_hidT(j - 1)
                if j >= 2:
                    finish(j - 2)

        @block.tensor
        def _(pe):
            ahead = Ahead()

            def multiply_chunk(n):
                half, c = divmod(n, NCH)
                if n == NCH:
                    pe.wait_ge(raw_done, 1)
                pe.wait_ge(masked, masked_count(n))
                v = chunk_view(n)
                for i, (t, k) in enumerate(rows_of(c)):
                    for s in range(2):
                        mm = nc.tensor.matmul(bank[0][s * B:(s + 1) * B, :], xT[0:k, t, :],
                                              v[0:k, s * NU:(s + 1) * NU, i, :],
                                              start=(t == GT - 1), stop=(t == GT - 2), tile_position=(0, s * B))
                mm.then_inc(used, 1)

            pe.wait_ge(x_in, 32)
            for n in range(NCH):
                if n == 5:
                    pe.wait_ge(const_pool, NCONST)
                    pe.wait_ge(small_in, 16 * 6)
                    nc.tensor.matmul(bank[3][:, 0:NX], mean_w[:], ws_sb[:], start=True, stop=True).then_inc(colmean_ps, 1)
                multiply_chunk(n)
            pe.wait_ge(bias_done, 1)
            pe.wait_ge(const_dve, 2)
            pe.wait_ge(wc_done, 1)

            for half in range(2):
                def after(stage):
                    for n in ahead.after(stage, half):
                        multiply_chunk(n)

                if half:
                    pe.wait_ge(h1T_done, half)
                for u in range(NU):
                    pe.wait_ge(xn_done, half * NU + u + 1)
                    mm = nc.tensor.transpose(bank[1][:, u * P:(u + 1) * P], xn[:, u, :], ident[:])
                mm.then_inc(xnT_ps, 1)
                after("norm")
                pe.wait_ge(xnT_done, half + 1)
                if half:
                    pe.wait_ge(att_done, 2 * HP)
                pe.wait_ge(wa_in, 16)
                for hp in range(HP):
                    nc.tensor.matmul(bank[4 + hp][:], wa_sb[:, hp * P:(hp + 1) * P], xnT[:], start=True, stop=True)\
                        .then_inc(gate_ps, 1)
                after("gates")
                pe.wait_ge(wv_in, 16)
                for u in range(NU):
                    i = half * NU + u
                    if u >= 2:
                        pe.wait_ge(v_done, i - 1)
                    elif half:
                        pe.wait_ge(h1_done if u == 0 else lm_done, half)
                    nc.tensor.matmul(bank[2 + u % 2][:], xnT[:, u * P:(u + 1) * P], wqkv_sb[:, 2 * INNER:3 * INNER],
                                     start=True, stop=False)
                    nc.tensor.matmul(bank[2 + u % 2][:], sel0[:], bias_b[:, BV], start=False, stop=True).then_inc(v_ps, 1)

                def keys_queries(hp):
                    i = half * HP + hp
                    if hp == 0:
                        pe.wait_ge(v_done, (half + 1) * NU)
                    else:
                        pe.wait_ge(k_raw, i)
                    nc.tensor.matmul(bank[2][:], wqkv_sb[:, INNER + hp * P:INNER + (hp + 1) * P], xnT[:],
                                     start=True, stop=True).then_inc(k_ps, 1)
                    if hp:
                        pe.wait_ge(q_raw, i)
                    nc.tensor.matmul(bank[3][:], wqkv_sb[:, hp * P:(hp + 1) * P], xnT[:],
                                     start=True, stop=True).then_inc(q_ps, 1)

                def scores(hp):
                    i = half * HP + hp
                    pe.wait_ge(k_done, i + 1)
                    pe.wait_ge(q_done, i + 1)
                    for key_half in range(half + 1):
                        n = sim_group(half, hp, key_half)
                        pe.wait_ge(gate_exp, HP * (half + 1))
                        if n >= 2:
                            pe.wait_ge(att_done, 2 * (n - 1))
                        for u in range(NU):
                            for odd in range(2):
                                r = slice(odd * DH, (odd + 1) * DH)
                                mm = nc.tensor.matmul(bank[4 + 2 * (n % 2) + odd][:, u * P:(u + 1) * P],
                                                      ks[r, key_half, hp, u * P:(u + 1) * P],
                                                      qs[r, i % 2, u * P:(u + 1) * P],
                                                      start=True, stop=True, tile_position=(odd * DH, 0))
                        mm.then_inc(sim_ps, 1)

                def mix(hp):
                    i = half * HP + hp
                    if hp == 0:
                        pe.wait_ge(xnT_done, half + 1)
                    else:
                        pe.wait_ge(ao_done, i)
                    pe.wait_ge(att_done, 2 * (sim_group(half, hp, half) + 1))
                    for u in range(NU):
                        for key_half in range(half + 1):
                            n = sim_group(half, hp, key_half)
                            for odd in range(2):
                                h = 2 * hp + odd
                                mm = nc.tensor.matmul(bank[1][odd * DH:(odd + 1) * DH, u * P:(u + 1) * P],
                                                      vv[:, key_half, u, h * DH:(h + 1) * DH],
                                                      att[:, n % 4, odd, u * P:(u + 1) * P],
                                                      start=(key_half == 0), stop=(key_half == half),
                                                      tile_position=(0, odd * DH))
                    mm.then_inc(ao_ps, 1)

                pe.wait_ge(wqk_in, 16)
                keys_queries(0)
                keys_queries(1)
                after("values")
                scores(0)
                after("first")
                for hp in range(HP):
                    if hp + 2 < HP:
                        keys_queries(hp + 2)
                    if hp + 1 < HP:
                        scores(hp + 1)
                    mix(hp)
                    after(f"pair{hp}")
                pe.wait_ge(wout_in, 16)
                pe.wait_ge(ao_done, HP * (half + 1))
                pe.wait_ge(k_raw, HP * (half + 1))
                nc.tensor.matmul(bank[2][:].rearrange("p (u d) -> p u d", u=NU), sel0[:],
                                 bias_b[:, BO].rearrange("p (a d) -> p a d", a=1).broadcast_to([3 * NX, NU, D]),
                                 start=True, stop=False)
                for u in range(NU):
                    for hp in range(HP):
                        mm = nc.tensor.matmul(bank[2][:, u * P:(u + 1) * P], aoT[:, hp, u * P:(u + 1) * P],
                                              wout_sb[:, hp, :], start=False, stop=(u == NU - 1 and hp == HP - 1))
                mm.then_inc(y_ps, 1)
                after("project")
                pe.wait_ge(h1_done, half + 1)
                for u in range(NU):
                    mm = nc.tensor.transpose(bank[1][:, u * P:(u + 1) * P], rows[:, half * NU + u, 0:D], ident[:])
                mm.then_inc(h1T_ps, 1)
                pe.wait_ge(h1T_done, half + 1)
                pe.wait_ge(q_raw, HP * (half + 1))
                for u in range(NU):
                    mm = nc.tensor.matmul(bank[3][:, u * NX:(u + 1) * NX], h1T[:, u * P:(u + 1) * P], wc_sb[:],
                                          start=True, stop=True)
                mm.then_inc(lg_ps, 1)
                after("route")

            pe.wait_ge(oh_done, 2)
            for t in range(NT):
                nc.tensor.matmul(bank[2][:, 0:NX], ones_bf[:], ohb[:, t, :], start=(t == 0), stop=(t == NT - 1))
            ohf = ohb[:].rearrange("p t x -> p (t x)")
            mm = nc.tensor.matmul(bank[3][:, 0:NT * NX], earlier[:], ohf, start=True, stop=False)
            for k in range(1, NT):
                mm = nc.tensor.matmul(bank[3][:, k * NX:NT * NX], ones_bf[:], ohf[:, 0:(NT - k) * NX],
                                      start=False, stop=(k == NT - 1))
            mm.then_inc(rank_ps, 1)

            pe.wait_ge(owner_done, 1)
            owner = [pe.value_load(owner_i[0:1, j:j + 1], min_val=0, max_val=NX - 1) for j in range(TILES)]
            pe.wait_ge(pick_done, 1)

            def transpose_rows(j):
                pe.wait_ge(sx_done, j + 1)
                if j >= 2:
                    pe.wait_ge(sxT_done, j - 1)
                nc.tensor.transpose(bank[j % 2][:, 0:P], sx[:, j % 4, :], ident[:]).then_inc(sxT_ps, 1)

            def expand(j):
                pe.wait_ge(sxT_done, j + 1)
                if j >= 2:
                    pe.wait_ge(hid_done, j - 1)
                o = bank[2 + j % 2][:]
                nc.tensor.matmul(o, sxT[:, j % 4, :], w1_sb[:, bass.ds(owner[j] * F, F)], start=True, stop=False)
                nc.tensor.matmul(o, pick[:, j, :], bias_b[:, B1], start=False, stop=True).then_inc(hid_ps, 1)

            def turn(j):
                pe.wait_ge(hid_done, j + 1)
                if j >= 2:
                    pe.wait_ge(hidT_done, j - 1)
                for c in range(FC):
                    mm = nc.tensor.transpose(bank[4 + j % 2][:, c * P:(c + 1) * P], hid[:, j % 2, c * P:(c + 1) * P],
                                             ident[:])
                mm.then_inc(hidT_ps, 1)

            def contract(j):
                pe.wait_ge(hidT_done, j + 1)
                if j >= 2:
                    pe.wait_ge(fin_done, j - 1)
                o = bank[6 + j % 2][:, 0:D]
                nc.tensor.matmul(o, pick[:, j, :], bias_b[:, B2], start=True, stop=False)
                for c in range(FC):
                    mm = nc.tensor.matmul(o, hidT[:, j % 2, c * P:(c + 1) * P],
                                          w2_sb[:, bass.ds(owner[j] * F + c * D, D)], start=False, stop=(c == FC - 1))
                mm.then_inc(ffn_ps, 1)

            pe.wait_ge(w1_in, 16)
            pe.wait_ge(w2_in, 16)
            transpose_rows(0)
            transpose_rows(1)
            for j in range(TILES + 1):
                if j < TILES:
                    expand(j)
                if j + 2 < TILES:
                    transpose_rows(j + 2)
                if j >= 1:
                    contract(j - 1)
                if j < TILES:
                    turn(j)


def kernel(x, L0_tok_weight, L0_tok_bias, L0_tok_mask, L0_attn_gamma, L0_attn_w_qkv, L0_attn_b_qkv, L0_attn_w_a,
           L0_attn_b_a, L0_attn_w_out, L0_attn_b_out, L0_ffn_Ws, L0_ffn_bs, L0_ffn_W1, L0_ffn_b1, L0_ffn_W2,
           L0_ffn_b2):
    import numpy as np
    import concourse.bacc as bacc
    from concourse.bass_utils import run_bass_kernel_spmd

    def by_partition(v):
        return np.ascontiguousarray(np.asarray(v).reshape(-1, P).T)

    bqkv = np.asarray(L0_attn_b_qkv)
    arrays = {
        "x_t": np.ascontiguousarray(np.asarray(x).T),
        "weight": np.asarray(L0_tok_weight),
        "tok_bias": np.asarray(L0_tok_bias),
        "mask": np.asarray(L0_tok_mask),
        "gamma": by_partition(L0_attn_gamma),
        "w_qkv": np.asarray(L0_attn_w_qkv),
        "bq": by_partition(bqkv[0:INNER]),
        "bk": by_partition(bqkv[INNER:2 * INNER]),
        "b_v": bqkv[2 * INNER:3 * INNER].reshape(1, INNER),
        "w_a": np.asarray(L0_attn_w_a),
        "ba": by_partition(L0_attn_b_a),
        "w_out": np.asarray(L0_attn_w_out),
        "b_out": np.asarray(L0_attn_b_out).reshape(1, D),
        "w_s": np.asarray(L0_ffn_Ws),
        "b_s": np.asarray(L0_ffn_bs).reshape(1, NX),
        "w1": np.asarray(L0_ffn_W1),
        "b1": np.asarray(L0_ffn_b1),
        "w2": np.asarray(L0_ffn_W2),
        "b2": np.asarray(L0_ffn_b2),
    }
    nc = bacc.Bacc("TRN2", target_bir_lowering=False, num_devices=1)
    feeds, aps = {}, {}
    for name, a in arrays.items():
        feeds[f"in_{name}"] = np.ascontiguousarray(a)
        aps[name] = nc.dram_tensor(f"in_{name}", a.shape, mybir.dt.from_np(a.dtype), kind="ExternalInput").ap()
    aps["out"] = nc.dram_tensor("out_tower", (B, E, D), F32, kind="ExternalOutput").ap()
    build(nc, **aps)
    r = run_bass_kernel_spmd(nc, [feeds], core_ids=[0])
    return r.results[0]["out_tower"]
```

```python
from contextlib import ExitStack

import concourse.bass as bass
from concourse import mybir

F32 = mybir.dt.float32
BF16 = mybir.dt.bfloat16
I32 = mybir.dt.int32
ALU = mybir.AluOpType
ACT = mybir.ActivationFunctionType
AX = mybir.AxisListType

P = 128
B = 64
E = 16
G = 5000
D = 128
HEADS = 8
DH = 64
INNER = HEADS * DH
HP = HEADS // 2
NX = 8
F = 512
FC = F // P
FB = F + FC
LN_EPS = 1e-5
NORM_FLOOR = 1e-12
SCALE = DH ** -0.5
A_FLOOR = 1e-10
INV_FLOOR = 1e-8

EH = E // 2
GT = G // P
GREM = G - GT * P
TC = 2
NCH = -(-(GT + 1) // TC)
SLOT = EH * TC * D
NSLOT = 5
UB = 16
GQ = P // 2
NU = B // UB
NT = 2 * NU
NTOK = B * E
HTOK = NTOK // 2
TILES = NTOK // P + NX - 1
REGION_TILES = NX * NU + NU + NX - 1
ROW = D + 4
V_DVE = 2
NCONST = 16
NO_TOKEN = 4096.0

PE_AHEAD = {"start": 1, "norm": 0, "gates": 4, "values": 2, "first": 1, "pair0": 2, "pair1": 1, "pair2": 3,
            "pair3": 2, "project": 2}
DVE_AHEAD = {"start": 1, "norm": 2, "clip0": 1, "scan0": 1, "clip1": 1, "scan1": 2, "first": 2, "pair0": 2,
             "pair1": 0, "pair2": 3, "pair3": 4, "project": 6}
WARM_NORM = 18
WARM_GATES = 4
WARM_FFN = 32
B2 = slice(0, D)
BV = slice(D, D + INNER)
BO = slice(D + INNER, D + INNER + D)
NBIAS = D + INNER + D


def build(nc, x_t, weight, tok_bias, mask, gamma, w_qkv, bq, bk, b_v, w_a, ba, w_out, b_out,
          w_s, b_s, w1, b1, w2, b2, out):
    ctx = ExitStack()
    with ctx:
        def sb(name, shape, dt=F32):
            return ctx.enter_context(nc.sbuf_tensor(name, shape, dt))

        def sem(name):
            return ctx.enter_context(nc.semaphore(name))

        xT = sb("xT", [P, GT + 1, B])
        maskt = sb("maskt", [P, GT + 1, D])
        ring = sb("ring", [P, NSLOT, SLOT])
        flat = ring[:, :, :].rearrange("p a b -> p (a b)")
        w1_sb = flat[:, 0:NX * FB].rearrange("p (e f) -> p e f", e=NX)
        w2_sb = flat[:, NX * FB:NX * (FB + F)]
        wqkv_sb = sb("wqkv_sb", [P, 3 * INNER])
        wa_sb = sb("wa_sb", [P, INNER])
        wout_sb = sb("wout_sb", [P, HP, D])
        gamma_sb = sb("gamma_sb", [P, 1])
        bq_sb = sb("bq_sb", [P, HP])
        bk_sb = sb("bk_sb", [P, HP])
        ba_sb = sb("ba_sb", [P, HP])
        nba_sb = sb("nba_sb", [P, HP])
        tokb_bc = sb("tokb_bc", [P, 2, NU * D])
        ws_sb = sb("ws_sb", [P, NX])
        bs_bc = sb("bs_bc", [P, NX])
        ident = sb("ident", [P, P])
        mean_w = sb("mean_w", [P, P])
        sel0 = sb("sel0", [3 * NX, P], BF16)
        ones_bf = sb("ones_bf", [P, P], BF16)
        earlier = sb("earlier", [P, P], BF16)
        keep = sb("keep", [P, P])
        keep_both = sb("keep_both", [P, 2, GQ])
        restart = sb("restart", [P, 2 * HTOK], BF16)
        pow_half = sb("pow_half", [P, 4])
        rev = sb("rev", [P, NX])
        steps = sb("steps", [P, NX])
        before = sb("before", [P, NX, NX])
        tile_no = sb("tile_no", [P, TILES])
        expert_no = sb("expert_no", [P, NX])
        room = sb("room", [P, NX])
        region = sb("region", [P, NX])
        shift = sb("shift", [P, NX])
        owner_r = sb("owner_r", [P, TILES])
        chosen = sb("chosen", [P, TILES, NX])
        unused = sb("unused", [P, TILES])
        place = sb("place", [P, TILES])
        place_i = sb("place_i", [P, TILES], I32)
        pidx = sb("pidx", [P, 1], I32)
        pidx8 = sb("pidx8", [P, 1], I32)
        pmod = sb("pmod", [P, 1], I32)
        pmod_f = sb("pmod_f", [P, 1])
        tok_f = sb("tok_f", [P, 2])
        token = sb("token", [P, NT])
        part = sb("part", [P, 4])
        zero_row = sb("zero_row", [P, ROW])
        hraw = sb("hraw", [P, NU, D])
        stats = sb("stats", [P, NU, 6])
        mv = sb("mv", [P, NU, 2])
        tiny = sb("tiny", [P, NU, 2])
        scale = sb("scale", [P, NU])
        xnT = sb("xnT", [P, HTOK])
        gl = sb("gl", [P, HP, HTOK])
        cum = sb("cum", [P, HP, HTOK])
        ginv = sb("ginv", [P, HP, HTOK])
        kraw = sb("kraw", [P, 2, HTOK])
        qraw = sb("qraw", [P, 2, HTOK])
        ks = sb("ks", [P, 2, HP, HTOK])
        qs = sb("qs", [P, 2, HTOK])
        vv = sb("vv", [P, NU, INNER])
        vv_both = sb("vv_both", [P, 2 * NU, INNER])
        att = sb("att", [P, 3, 2, HTOK])
        xn = att[:, 2, 0, :].rearrange("p (u d) -> p u d", u=NU)
        aoT = sb("aoT", [P, HP, HTOK])
        rows = sb("rows", [P, NT, ROW])
        h1T = xnT
        wc_sb = sb("wc_sb", [P, NX])
        lg = sb("lg", [P, NU, NX])
        mx = sb("mx", [P, NU])
        cand = sb("cand", [P, NU, NX])
        cm = sb("cm", [P, NT])
        ex = sb("ex", [P, NU, NX])
        esum = sb("esum", [P, NU])
        ohb = sb("ohb", [P, NT, NX], BF16)
        rank = sb("rank", [P, NU, NX])
        cmp = sb("cmp", [P, NX, NX])
        ntile = sb("ntile", [P, NX])
        first = sb("first", [P, NX])
        last = sb("last", [P, NX])
        slot_f = sb("slot_f", [P, NT])
        slot_i = sb("slot_i", [P, NT], I32)
        owner_c = sb("owner_c", [P, TILES, NX])
        owner_f = sb("owner_f", [P, TILES])
        owner_i = sb("owner_i", [P, TILES], I32)
        bias_f = aoT[0:3 * NX, :, :].rearrange("p a b -> p (a b)")[:, 0:NBIAS]
        bias_r = att[0:3 * NX, 0:2, :, :].rearrange("p a b c -> p (a b c)")[:, 0:NBIAS]
        bias_p = [b[0:3 * NX, 0:2, :].rearrange("p a b -> p (a b)").bitcast(BF16)[:, 0:NBIAS] for b in (gl, cum, ginv)]
        bias_b = sb("bias_b", [3 * NX, NBIAS], BF16)
        pick = sb("pick", [3 * NX, TILES, P], BF16)
        srow = ks[:, :, :, :].rearrange("p a b c -> p (a b c)")[:, 0:TILES * ROW].rearrange("p (t r) -> p t r", r=ROW)
        sx = gl[:, 0, :].rearrange("p (a b) -> p a b", a=4)
        sxT = gl[:, 1, :].rearrange("p (a b) -> p a b", a=4)
        hid = cum[:, 0:2, :]
        w1_now = att[:, :, :, :].rearrange("p a b c -> p (a b c)")[:, 0:3 * FB].rearrange("p (a f) -> p a f", a=3)
        w2_now = [cum[:, 2, :], cum[:, 3, :], qs[:, 1, :]]
        fin = ginv[:, 0, :].rearrange("p (a b) -> p a b", a=4)
        fin0 = ginv[:, 1, :].rearrange("p (a b) -> p a b", a=4)
        dest = sb("dest", [P, TILES], I32)

        bank = [ctx.enter_context(nc.psum_tensor(f"bank{i}", [P, 512], F32)) for i in range(8)]
        h_rows = nc.dram_tensor("h_rows", [2, B, EH * D], F32, kind="Internal").ap()
        sorted_rows = nc.dram_tensor("sorted_rows", [(REGION_TILES + 1) * P, ROW], F32, kind="Internal").ap()

        slot_in = [sem(f"slot_in{i}") for i in range(NSLOT)]
        x_in = sem("x_in")
        tokb_in = [sem("tokb_in0"), sem("tokb_in1")]
        small_in = sem("small_in")
        bias_in = sem("bias_in")
        bias_done = sem("bias_done")
        wa_in = sem("wa_in")
        wv_in = sem("wv_in")
        wqk_in = sem("wqk_in")
        wout_in = sem("wout_in")
        w1_in = sem("w1_in")
        w2_in = sem("w2_in")
        h_out = sem("h_out")
        res_in = sem("res_in")
        zeroed = sem("zeroed")
        spread = sem("spread")
        srow_in = [sem(f"srow_in{i}") for i in range(4)]
        stored = [sem(f"stored{i}") for i in range(4)]
        const_pool = sem("const_pool")
        pool_step = sem("pool_step")
        dve_step = sem("dve_step")
        const_dve = sem("const_dve")
        masked = sem("masked")
        used = sem("used")
        raw_done = sem("raw_done")
        var_done = sem("var_done")
        scale_done = sem("scale_done")
        xn_done = sem("xn_done")
        xnT_ps = sem("xnT_ps")
        xnT_done = sem("xnT_done")
        gate_ps = sem("gate_ps")
        gate_exp = sem("gate_exp")
        gate_clip = sem("gate_clip")
        gate_ln = sem("gate_ln")
        gate_cum = sem("gate_cum")
        gate_cap = sem("gate_cap")
        gate_a = sem("gate_a")
        gate_inv = sem("gate_inv")
        v_ps = sem("v_ps")
        v_done = sem("v_done")
        v_even_done = sem("v_even_done")
        vv_moved = sem("vv_moved")
        k_ps = sem("k_ps")
        k_raw = sem("k_raw")
        q_raw = sem("q_raw")
        k_done = sem("k_done")
        q_ps = sem("q_ps")
        q_done = sem("q_done")
        sim_ps = sem("sim_ps")
        att_zeroed = sem("att_zeroed")
        att_done = sem("att_done")
        ao_ps = sem("ao_ps")
        ao_done = sem("ao_done")
        y_ps = sem("y_ps")
        h1_done = sem("h1_done")
        var2_done = sem("var2_done")
        scale2_done = sem("scale2_done")
        h1T_ps = sem("h1T_ps")
        h1T_done = sem("h1T_done")
        colmean_ps = sem("colmean_ps")
        wc_done = sem("wc_done")
        lg_ps = sem("lg_ps")
        lm_done = sem("lm_done")
        ex_done = sem("ex_done")
        oh_done = sem("oh_done")
        rank_ps = sem("rank_ps")
        cnt_ps = sem("cnt_ps")
        slot_done = sem("slot_done")
        owner_done = sem("owner_done")
        place_done = sem("place_done")
        pick_done = sem("pick_done")
        sx_done = sem("sx_done")
        sxT_ps = sem("sxT_ps")
        sxT_done = sem("sxT_done")
        hid_ps = sem("hid_ps")
        hid_done = sem("hid_done")
        w_now = sem("w_now")
        ffn_ps = sem("ffn_ps")
        fin_done = sem("fin_done")
        dest_done = sem("dest_done")

        block = ctx.enter_context(nc.Block())

        def rows_of(c):
            ts = (GT - 1, GT) if c == 0 else range(TC * (c - 1), TC * c)
            return [(t, P if t < GT else GREM) for t in ts]

        def slot_in_count(n):
            total = 0
            for m in range(n % NSLOT, n + 1, NSLOT):
                h, c = divmod(m, NCH)
                dmas = 2 if c == 0 else 1
                total += 16 * dmas * (2 if h == 0 else 1)
            return total

        def chunk_view(n):
            return ring[:, n % NSLOT, :].rearrange("p (e t d) -> p e t d", e=EH, t=TC)

        w_main = weight[:, 0:GT * P, :].rearrange("e (p t) d -> p e t d", t=GT)
        w_rest = weight[:, GT * P:G, :].rearrange("e p d -> p e d")
        m_main = mask[0:GT * P, :].rearrange("(p t) d -> p t d", t=GT)
        m_rest = mask[GT * P:G, :]
        x_main = x_t[0:GT * P, :].rearrange("(p t) b -> p t b", t=GT)
        x_rest = x_t[GT * P:G, :]

        class Ahead:

            def __init__(self, table):
                self.table = table
                self.next = NCH

            def after(self, stage, half):
                n0 = self.next
                if half == 0:
                    count = self.table[stage] if stage != "route" else 2 * NCH - n0
                    self.next = min(2 * NCH, n0 + count)
                return range(n0, self.next)

        def sums(half):
            return bank[1 - half]

        def att_slot(i):
            return i % 2 if i < HP else i % 3

        def att_count(i):
            return 4 * min(i, HP) + 2 * max(i - HP, 0)

        def value_bank(half, u):
            return bank[(2, 3, 1, 0)[u]] if half else bank[2 + u % 2]

        def load_token_bias(engine, half):
            for s in range(2):
                e0 = half * EH + s * NU
                src = tok_bias[e0:e0 + NU, :].rearrange("(a e) d -> a (e d)", a=1)
                engine.dma_start(tokb_bc[s * B:(s + 1) * B, half, :], src.broadcast_to([B, NU * D]))\
                    .then_inc(tokb_in[half], 16)

        @block.sync
        def _(sp):
            def load_chunk(n):
                half, c = divmod(n, NCH)
                s = slot_in[n % NSLOT]
                if n >= NSLOT:
                    sp.wait_ge(used, n - NSLOT + 1)
                ts = [t for t, k in rows_of(c) if k == P]
                t0, t1 = ts[0], ts[-1] + 1
                v = chunk_view(n)
                if half == 0:
                    sp.dma_start(maskt[:, t0:t1, :], m_main[:, t0:t1, :]).then_inc(s, 16)
                sp.dma_start(v[:, :, 0:t1 - t0, :], w_main[:, half * EH:(half + 1) * EH, t0:t1, :]).then_inc(s, 16)
                if c == 0:
                    if half == 0:
                        sp.dma_start(maskt[0:GREM, GT, :], m_rest).then_inc(s, 16)
                    sp.dma_start(v[0:GREM, :, 1, :], w_rest[:, half * EH:(half + 1) * EH, :]).then_inc(s, 16)

            for n in range(2 * NCH):
                load_chunk(n)
                if n == 0:
                    sp.dma_start(xT[0:GREM, GT, :], x_rest).then_inc(x_in, 16)
                    sp.dma_start(xT[:, 0:GT, :], x_main).then_inc(x_in, 16)
                if n == NCH - 1:
                    sp.dma_start(wa_sb[:], w_a).then_inc(wa_in, 16)
                    sp.dma_start(wqkv_sb[:, 2 * INNER:3 * INNER], w_qkv[:, 2 * INNER:3 * INNER]).then_inc(wv_in, 16)
                if n == NCH:
                    sp.dma_start(wqkv_sb[:, 0:2 * INNER], w_qkv[:, 0:2 * INNER]).then_inc(wqk_in, 16)
                    sp.dma_start(wout_sb[:], w_out.rearrange("(c p) d -> p c d", p=P)).then_inc(wout_in, 16)
                if n == NCH + 6:
                    load_token_bias(sp, 1)
                if n == 2 * NCH - 1:
                    sp.wait_ge(const_pool, NCONST)
                    sp.dma_start(sorted_rows.rearrange("(t p) r -> p t r", p=P),
                                 zero_row[:].rearrange("p (a r) -> p a r", a=1).broadcast_to([P, REGION_TILES + 1, ROW]))\
                        .then_inc(zeroed, 16)
            sp.wait_ge(used, 2 * NCH)
            sp.dma_start(w1_sb[:, :, F:FB], b1.rearrange("e (p c) -> p e c", c=FC)).then_inc(w1_in, 16)
            sp.dma_start(w1_sb[:, :, 0:F], w1.rearrange("e d f -> d e f")).then_inc(w1_in, 16)
            sp.dma_start(w2_sb.rearrange("p (e f) -> p e f", e=NX),
                         w2.rearrange("e (p c) d -> p e (c d)", c=FC)).then_inc(w2_in, 16)
            sp.wait_ge(place_done, 1)

            def first_row_of(j):
                return sp.value_load(place_i[0:1, j:j + 1], min_val=0, max_val=REGION_TILES * P)

            known = [first_row_of(j) for j in range(3)]
            sp.wait_ge(spread, 16 * NT)
            sp.wait_ge(ao_ps, 2 * HP)
            for j in range(TILES):
                first_row = known[j] if j < len(known) else first_row_of(j)
                if j >= 4:
                    sp.wait_ge(srow_in[j % 4], 16 * (j // 4))
                sp.dma_start(srow[:, j, :], sorted_rows[bass.ds(first_row, P), :]).then_inc(srow_in[j % 4], 16)

        @block.gpsimd
        def _(pool):
            count = [0]

            def link(ins):
                count[0] += 1
                ins.then_inc(pool_step, 1)
                pool.wait_ge(pool_step, count[0])

            link(nc.gpsimd.memset(ident[:], 0.0))
            nc.gpsimd.affine_select(out=ident[:], in_=ident[:], compare_op=ALU.not_equal, fill=1.0, base=0,
                                    pattern=[[-1, P]], channel_multiplier=1).then_inc(const_pool, 1)
            nc.gpsimd.memset(ones_bf[:], 1.0).then_inc(const_pool, 1)
            nc.gpsimd.memset(pow_half[:], -0.5).then_inc(const_pool, 1)
            link(nc.gpsimd.memset(earlier[:], 1.0))
            nc.gpsimd.affine_select(out=earlier[:], in_=earlier[:], compare_op=ALU.is_gt, fill=0.0, base=0,
                                    pattern=[[1, P]], channel_multiplier=-1).then_inc(const_pool, 1)
            link(nc.gpsimd.memset(keep[:], SCALE))
            v = keep[:].rearrange("p (b e) -> p b e", e=EH)
            link(nc.gpsimd.affine_select(out=v, in_=v, compare_op=ALU.is_ge, fill=0.0, base=0,
                                         pattern=[[-EH, UB], [0, EH]], channel_multiplier=1))
            link(nc.gpsimd.affine_select(out=v, in_=v, compare_op=ALU.is_ge, fill=0.0, base=EH - 1,
                                         pattern=[[EH, UB], [0, EH]], channel_multiplier=-1))
            nc.gpsimd.affine_select(out=keep[:], in_=keep[:], compare_op=ALU.is_ge, fill=0.0, base=0,
                                    pattern=[[1, P]], channel_multiplier=-1).then_inc(const_pool, 1)
            link(nc.gpsimd.memset(keep_both[:], SCALE))
            for s in range(2):
                r = slice(s * GQ, (s + 1) * GQ)
                v = keep_both[r, :, :].rearrange("p m (b e) -> p m b e", e=EH)
                link(nc.gpsimd.affine_select(out=v, in_=v, compare_op=ALU.is_ge, fill=0.0, base=0,
                                             pattern=[[0, 2], [-EH, GQ // EH], [0, EH]], channel_multiplier=1))
                link(nc.gpsimd.affine_select(out=v, in_=v, compare_op=ALU.is_ge, fill=0.0, base=EH - 1,
                                             pattern=[[0, 2], [EH, GQ // EH], [0, EH]], channel_multiplier=-1))
                v = keep_both[r, 1 - s, :]
                link(nc.gpsimd.affine_select(out=v, in_=v, compare_op=ALU.is_ge, fill=0.0, base=0,
                                             pattern=[[1, GQ]], channel_multiplier=-1))
            link(nc.gpsimd.memset(restart[:], 1.0))
            nc.gpsimd.memset(restart[:].rearrange("p (b e) -> p b e", e=EH)[:, :, 0:1], 0.0).then_inc(const_pool, 1)
            small = dict(allow_small_or_imprecise_dtypes=True)
            nc.gpsimd.iota(rev[:], [[-1, NX]], base=NX, channel_multiplier=0, **small).then_inc(const_pool, 1)
            nc.gpsimd.iota(steps[:], [[P, NX]], base=0, channel_multiplier=0, **small).then_inc(const_pool, 1)
            nc.gpsimd.iota(tile_no[:], [[1, TILES]], base=0, channel_multiplier=0, **small).then_inc(const_pool, 1)
            nc.gpsimd.iota(expert_no[:], [[1, NX]], base=0, channel_multiplier=0, **small).then_inc(const_pool, 1)
            nc.gpsimd.iota(room[:], [[NU, NX]], base=0, channel_multiplier=0, **small).then_inc(const_pool, 1)
            nc.gpsimd.iota(pidx[:], [[0, 1]], base=0, channel_multiplier=1).then_inc(const_pool, 1)
            link(nc.gpsimd.memset(before[:], 1.0))
            nc.gpsimd.affine_select(out=before[:], in_=before[:], compare_op=ALU.is_gt, fill=0.0, base=0,
                                    pattern=[[1, NX], [-1, NX]], channel_multiplier=0).then_inc(const_pool, 1)
            link(nc.gpsimd.memset(part[:], 1.0))
            link(nc.gpsimd.affine_select(out=part[:, 0:3], in_=part[:, 0:3], compare_op=ALU.is_ge, fill=0.0, base=0,
                                         pattern=[[-NX, 3]], channel_multiplier=1))
            nc.gpsimd.affine_select(out=part[:, 0:3], in_=part[:, 0:3], compare_op=ALU.is_ge, fill=0.0, base=NX - 1,
                                    pattern=[[NX, 3]], channel_multiplier=-1).then_inc(const_pool, 1)
            nc.gpsimd.memset(zero_row[:], 0.0).then_inc(const_pool, 1)
            nc.gpsimd.memset(mean_w[:], 1.0 / D).then_inc(const_pool, 1)

            pool.wait_ge(bias_done, 1)
            nc.gpsimd.memset(att[:, 0:2, :, :].rearrange("p a b c -> p (a b c)"), 0.0).then_inc(att_zeroed, 1)

            def spread_half(half):
                pool.wait_ge(slot_done, half + 1)
                pool.wait_ge(zeroed, 16)
                for t in range(half * NU, (half + 1) * NU):
                    pool.indirect_dma_start(out=sorted_rows,
                                            out_offset=bass.IndirectOffsetOnAxis(ap=slot_i[:, t:t + 1], axis=0),
                                            in_=rows[:, t, :], in_offset=None).then_inc(spread, 16)

            for half in range(2):
                pool.wait_ge(var_done, half + 1)
                nc.gpsimd.tensor_tensor(scale[:], tiny[:, :, 1], pow_half[:], ALU.pow).then_inc(scale_done, 1)
                pool.wait_ge(raw_done, half + 1)
                for s in range(2):
                    pool.dma_start(h_rows[half, :, s * NU * D:(s + 1) * NU * D],
                                   hraw[s * B:(s + 1) * B, :, :].rearrange("p u d -> p (u d)")).then_inc(h_out, 16)
                pool.wait_ge(h_out, 32 * (half + 1))
                pool.dma_start(rows[:, half * NU:(half + 1) * NU, 0:D],
                               h_rows[half].rearrange("(u c) (e d) -> (c e) u d", c=UB, e=EH)).then_inc(res_in, 16)
                if half == 0:
                    pool.wait_ge(v_done, NU)
                    for s in range(2):
                        pr = slice(s * GQ, (s + 1) * GQ)
                        pool.dma_start(vv_both[pr, :, :].rearrange("p (u s) c -> p u s c", s=2)[:, :, s, :], vv[pr, :, :])\
                            .then_inc(vv_moved, 16)
                if half:
                    spread_half(0)
                pool.wait_ge(var2_done, half + 1)
                nc.gpsimd.tensor_tensor(scale[:], tiny[:, :, 1], pow_half[:], ALU.pow).then_inc(scale2_done, 1)
            spread_half(1)
            pool.wait_ge(owner_done, 1)
            nc.gpsimd.tensor_scalar(pick[:], owner_f[0:3 * NX, :].rearrange("p (t a) -> p t a", a=1)
                                    .broadcast_to([3 * NX, TILES, P]), pmod_f[0:3 * NX, 0:1], None, ALU.is_equal)\
                .then_inc(pick_done, 1)
            out_rows = out.rearrange("b e d -> (b e) d")
            for j in range(TILES):
                pool.wait_ge(fin_done, j + 1)
                pool.wait_ge(dest_done, j + 1)
                pool.indirect_dma_start(out=out_rows, out_offset=bass.IndirectOffsetOnAxis(ap=dest[:, j:j + 1], axis=0),
                                        in_=fin[:, j % 4, :], in_offset=None,
                                        bounds_check=NTOK - 1, oob_is_err=False).then_inc(stored[j % 4], 16)
            for k in range(4):
                pool.wait_ge(stored[k], 16 * len(range(k, TILES, 4)))

        @block.scalar
        def _(act):
            load_token_bias(act, 0)
            for dst, src in ((gamma_sb[:], gamma), (bq_sb[:], bq), (bk_sb[:], bk), (ba_sb[:], ba), (ws_sb[:], w_s),
                             (bs_bc[:], b_s.broadcast_to([P, NX]))):
                act.dma_start(dst, src).then_inc(small_in, 16)
            for i in range(3):
                act.dma_start(bias_f[i * NX:(i + 1) * NX, B2], b2).then_inc(bias_in, 16)
            act.dma_start(bias_f[:, BV], b_v.broadcast_to([3 * NX, INNER])).then_inc(bias_in, 16)
            act.dma_start(bias_f[:, BO], b_out.broadcast_to([3 * NX, D])).then_inc(bias_in, 16)
            act.preload_act_table_set("natural_log_exp_and_others")
            act.wait_ge(small_in, 16 * 6)
            act.wait_ge(const_dve, 1)
            for half in range(2):
                act.wait_ge(xnT_ps, half + 1)
                if half:
                    act.wait_ge(lg_ps, half)
                nc.scalar.activation(xnT[:].rearrange("p (b s e) -> p e s b", s=2, e=NU),
                                     bank[1][:].rearrange("p (e s b) -> p e s b", s=2, b=B),
                                     ACT.Copy, scale=gamma_sb[:, 0:1]).then_inc(xnT_done, 1)

                def gate(g):
                    act.wait_ge(gate_cum, 2 * half + g + 1)
                    nc.scalar.activation(gl[:, 2 * g:2 * g + 2, :], cum[:, 2 * g:2 * g + 2, :], ACT.Exp, scale=-1.0)\
                        .then_inc(gate_a, 1)
                    act.wait_ge(gate_cap, 2 * half + g + 1)
                    nc.scalar.activation(ginv[:, 2 * g:2 * g + 2, :], ginv[:, 2 * g:2 * g + 2, :], ACT.Exp)\
                        .then_inc(gate_inv, 1)

                def gate_log(g):
                    act.wait_ge(gate_clip, 2 * half + g + 1)
                    nc.scalar.activation(gl[:, 2 * g:2 * g + 2, :], gl[:, 2 * g:2 * g + 2, :], ACT.Ln)\
                        .then_inc(gate_ln, 1)

                def values(u):
                    act.wait_ge(v_ps, half * NU + u + 1)
                    if half:
                        nc.scalar.activation(vv_both[0:GQ, 2 * u + 1, :], value_bank(1, u)[0:GQ, :], ACT.Copy)\
                            .then_inc(v_done, 1)
                        if u >= V_DVE:
                            nc.scalar.activation(vv_both[GQ:P, 2 * u, :], value_bank(1, u)[GQ:P, :], ACT.Copy)\
                                .then_inc(v_done, 1)
                    else:
                        nc.scalar.activation(vv[:, u, :], value_bank(0, u)[:], ACT.Copy).then_inc(v_done, 1)

                def key_query(hp):
                    i = half * HP + hp
                    act.wait_ge(k_ps, i + 1)
                    if i >= 2:
                        act.wait_ge(k_done, i - 1)
                    nc.scalar.activation(kraw[:, i % 2, :], bank[2][:], ACT.Identity, bias=bk_sb[:, hp:hp + 1])\
                        .then_inc(k_raw, 1)
                    act.wait_ge(q_ps, i + 1)
                    if i >= 2:
                        act.wait_ge(q_done, i - 1)
                    nc.scalar.activation(qraw[:, i % 2, :], bank[3][:], ACT.Identity, bias=bq_sb[:, hp:hp + 1])\
                        .then_inc(q_raw, 1)

                def gate_sum(hp):
                    act.wait_ge(gate_ps, half * HP + hp + 1)
                    if half and hp == 0:
                        act.wait_ge(q_done, HP)
                    if half == 0 and hp == 0:
                        act.wait_ge(bias_done, 1)
                    nc.scalar.activation(gl[:, hp, :], bank[4 + hp][:], ACT.Exp, scale=-1.0,
                                         bias=nba_sb[:, hp:hp + 1]).then_inc(gate_exp, 1)

                gate_sum(0)
                gate_sum(1)
                key_query(0)
                gate_log(0)
                gate_sum(2)
                gate_sum(3)
                key_query(1)
                if half:
                    gate(0)
                    gate_log(1)
                    values(0)
                    values(1)
                    values(2)
                    values(3)
                    gate(1)
                else:
                    gate(0)
                    gate_log(1)
                    for u in range(NU):
                        values(u)
                    gate(1)
                for hp in range(HP):
                    if hp + 2 < HP:
                        key_query(hp + 2)
                    i = half * HP + hp
                    act.wait_ge(ao_ps, i + 1)
                    if half and hp == 0:
                        act.wait_ge(y_ps, half)
                    nc.scalar.activation(aoT[:, hp, :], bank[1][:], ACT.Copy).then_inc(ao_done, 1)
                act.wait_ge(h1T_ps, half + 1)
                nc.scalar.activation(h1T[:], bank[1][:], ACT.Copy).then_inc(h1T_done, 1)
                act.wait_ge(lm_done, half + 1)
                nc.scalar.activation(ex[:], lg[:], ACT.Exp).then_inc(ex_done, 1)
            act.preload_act_table_set("gelu_and_others")

            def take_xT(j):
                act.wait_ge(sxT_ps, j + 1)
                if j >= 4:
                    act.wait_ge(hid_ps, j - 3)
                nc.scalar.activation(sxT[:, j % 4, :], bank[j % 2][:, 0:P], ACT.Copy).then_inc(sxT_done, 1)

            take_xT(0)
            take_xT(1)
            for j in range(TILES):
                act.wait_ge(hid_ps, j + 1)
                if j >= 2:
                    act.wait_ge(ffn_ps, j - 1)
                for c in range(FC):
                    o = slice(c * P, (c + 1) * P)
                    nc.scalar.activation(hid[:, j % 2, o], bank[2 + j % 2][:, o], ACT.Gelu,
                                         bias=w1_now[:, j % 3, F + c:F + c + 1]).then_inc(hid_done, 1)
                if j + 2 < TILES:
                    take_xT(j + 2)

        @block.vector
        def _(dve):
            count = [0]
            ahead = Ahead(DVE_AHEAD)

            def link(ins):
                count[0] += 1
                ins.then_inc(dve_step, 1)
                dve.wait_ge(dve_step, count[0])

            def mask_chunk(n):
                half, c = divmod(n, NCH)
                dve.wait_ge(slot_in[n % NSLOT], slot_in_count(n))
                v = chunk_view(n)
                for r, (t, k) in enumerate(rows_of(c)):
                    nc.vector.tensor_tensor(v[0:k, :, r, :], v[0:k, :, r, :],
                                            maskt[0:k, t:t + 1, :].broadcast_to([k, EH, D]), ALU.mult)\
                        .then_inc(masked, 1)

            def moments(src, s6):
                for u in range(NU):
                    ins = nc.vector.bn_stats(s6[:, u, :], src(u))
                    if u == NU - 1:
                        link(ins)
                    else:
                        ins.then_inc(dve_step, 1)
                        count[0] += 1
                for u in range(NU):
                    ins = nc.vector.bn_aggr(mv[:, u, :], s6[:, u, :])
                    if u == NU - 1:
                        link(ins)
                    else:
                        ins.then_inc(dve_step, 1)
                        count[0] += 1

            def constants():
                dve.wait_ge(const_pool, NCONST)
                link(nc.vector.tensor_single_scalar(pidx8[:], pidx[:], -EH, ALU.bitwise_and))
                link(nc.vector.tensor_single_scalar(pmod[:], pidx[:], NX - 1, ALU.bitwise_and))
                link(nc.vector.tensor_copy(pmod_f[:], pmod[:]))
                link(nc.vector.tensor_copy(tok_f[:, 0:1], pidx[:]))
                link(nc.vector.tensor_copy(tok_f[:, 1:2], pidx8[:]))
                link(nc.vector.tensor_tensor(tok_f[:, 0:1], tok_f[:, 0:1], tok_f[:, 1:2], ALU.add))
                for t in range(NT):
                    half, u = divmod(t, NU)
                    link(nc.vector.tensor_scalar_add(rows[:, t, D + 3:D + 4], tok_f[:, 0:1],
                                                     float(u * UB * E + half * EH) - NO_TOKEN))
                dve.wait_ge(small_in, 16 * 6)
                nc.vector.tensor_scalar_mul(nba_sb[:], ba_sb[:], -1.0).then_inc(const_dve, 1)
                nc.vector.tensor_scalar(sel0[:], ones_bf[0:3 * NX, :], 0.0, pmod_f[0:3 * NX, 0:1], ALU.mult,
                                        ALU.is_equal).then_inc(const_dve, 1)

            def bias_parts(step):
                if step == 0:
                    dve.wait_ge(bias_in, 16 * 5)
                    link(nc.vector.tensor_copy(bias_p[0], bias_f))
                    link(nc.vector.tensor_tensor(bias_r, bias_f, bias_p[0], ALU.subtract))
                elif step == 1:
                    link(nc.vector.tensor_copy(bias_p[1], bias_r))
                    link(nc.vector.tensor_tensor(bias_p[2], bias_r, bias_p[1], ALU.subtract))
                elif step == 2:
                    link(nc.vector.tensor_scalar(bias_r, bias_p[0], part[0:3 * NX, 0:1], None, ALU.mult))
                    link(nc.vector.scalar_tensor_tensor(bias_r, bias_p[1], part[0:3 * NX, 1:2], bias_r,
                                                        ALU.mult, ALU.add))
                else:
                    nc.vector.scalar_tensor_tensor(bias_b[:], bias_p[2], part[0:3 * NX, 2:3], bias_r,
                                                   ALU.mult, ALU.add).then_inc(bias_done, 1)

            for n in range(NCH):
                if n == 3:
                    constants()
                if 6 <= n < 10:
                    bias_parts(n - 6)
                if n == 11:
                    dve.wait_ge(colmean_ps, 1)
                    nc.vector.tensor_tensor(wc_sb[:], ws_sb[:], bank[3][:, 0:NX], ALU.subtract).then_inc(wc_done, 1)
                mask_chunk(n)

            def tiles_before(dst):
                link(nc.vector.tensor_tensor(cmp[:], bank[2][:, 0:NX].rearrange("p (x a) -> p x a", a=1).broadcast_to([P, NX, NX]),
                                             steps[:].rearrange("p (a k) -> p a k", a=1).broadcast_to([P, NX, NX]), ALU.is_gt))
                link(nc.vector.tensor_reduce(ntile[:], cmp[:], AX.X, ALU.add))
                link(nc.vector.tensor_tensor(cmp[:], before[:],
                                             ntile[:].rearrange("p (a k) -> p a k", a=1).broadcast_to([P, NX, NX]), ALU.mult))
                link(nc.vector.tensor_reduce(dst[:], cmp[:], AX.X, ALU.add))

            def slots(half):
                ts = slice(half * NU, (half + 1) * NU)
                dve.wait_ge(rank_ps, half + 1)
                link(nc.vector.scalar_tensor_tensor(rank[:], region[:].rearrange("p (a x) -> p a x", a=1).broadcast_to([P, NU, NX]),
                                                    float(P), bank[3][:, 0:NU * NX].rearrange("p (t x) -> p t x", t=NU),
                                                    ALU.mult, ALU.add))
                link(nc.vector.tensor_tensor(rank[:], rank[:], ohb[:, ts, :], ALU.mult))
                link(nc.vector.tensor_reduce(slot_f[:, ts], rank[:], AX.X, ALU.add))
                nc.vector.tensor_copy(slot_i[:, ts], slot_f[:, ts]).then_inc(slot_done, 1)

            for half in range(2):
                def after(stage):
                    for n in ahead.after(stage, half):
                        mask_chunk(n)

                after("start")
                dve.wait_ge(used, NCH * (half + 1))
                if half:
                    dve.wait_ge(h_out, 32)
                dve.wait_ge(tokb_in[half], 32)
                nc.vector.tensor_tensor(hraw[:].rearrange("p u d -> p (u d)"), sums(half)[:], tokb_bc[:, half, :],
                                        ALU.add).then_inc(raw_done, 1)
                dve.wait_ge(raw_done, half + 1)
                moments(lambda u: hraw[:, u, :], stats)
                floor = NORM_FLOOR ** 2 / D
                link(nc.vector.tensor_scalar(tiny[:, :, 0], mv[:, :, 1], LN_EPS, floor, ALU.add, ALU.mult))
                nc.vector.tensor_tensor(tiny[:, :, 1], mv[:, :, 1], tiny[:, :, 0], ALU.max).then_inc(var_done, 1)
                dve.wait_ge(scale_done, half + 1)
                for u in range(NU):
                    nc.vector.tensor_scalar(xn[:, u, :], hraw[:, u, :], mv[:, u, 0:1], scale[:, u:u + 1],
                                            ALU.subtract, ALU.mult).then_inc(xn_done, 1)
                if half:
                    dve.wait_ge(cnt_ps, 1)
                    tiles_before(region)
                    link(nc.vector.tensor_tensor(region[:], region[:], room[:], ALU.add))
                    slots(0)
                after("norm")
                def clip(g):
                    gs = gl[:, 2 * g:2 * g + 2, :]
                    dve.wait_ge(gate_exp, half * HP + 2 * g + 2)
                    nc.vector.tensor_scalar(gs, gs, 1.0, 1.0 / A_FLOOR, ALU.add, ALU.min).then_inc(gate_clip, 1)

                def scan(g):
                    gs = gl[:, 2 * g:2 * g + 2, :]
                    cs = cum[:, 2 * g:2 * g + 2, :]
                    dve.wait_ge(gate_ln, 2 * half + g + 1)
                    if half:
                        gv = gs.rearrange("p c (b e) -> p c b e", e=EH)[:, :, :, 0]
                        cv = cs.rearrange("p c (b e) -> p c b e", e=EH)[:, :, :, EH - 1]
                        dve.wait_ge(gate_cum, 2)
                        link(nc.vector.tensor_tensor(gv, gv, cv, ALU.add))
                        dve.wait_ge(gate_a, 2)
                    nc.vector.tensor_tensor_scan(cs.rearrange("p c t -> p (c t)"), restart[:],
                                                 gs.rearrange("p c t -> p (c t)"), 0.0, ALU.mult, ALU.add)\
                        .then_inc(gate_cum, 1)
                    dve.wait_ge(gate_cum, 2 * half + g + 1)
                    if half:
                        dve.wait_ge(k_done, HP)
                    nc.vector.tensor_scalar_min(ginv[:, 2 * g:2 * g + 2, :], cs, 40.0).then_inc(gate_cap, 1)

                def scaled_key_query(hp):
                    i = half * HP + hp
                    dve.wait_ge(k_raw, i + 1)
                    dve.wait_ge(gate_inv, 2 * half + hp // 2 + 1)
                    nc.vector.scalar_tensor_tensor(ks[:, half, hp, :], ginv[:, hp, :], 1.0 / INV_FLOOR, kraw[:, i % 2, :],
                                                   ALU.min, ALU.mult).then_inc(k_done, 1)
                    dve.wait_ge(q_raw, i + 1)
                    if i >= 2:
                        dve.wait_ge(sim_ps, i - 1)
                    nc.vector.tensor_tensor(qs[:, i % 2, :], qraw[:, i % 2, :], gl[:, hp, :], ALU.mult).then_inc(q_done, 1)

                def mask_scores(hp):
                    i = half * HP + hp
                    dve.wait_ge(sim_ps, i + 1)
                    if half == 0 and hp >= 2:
                        dve.wait_ge(ao_ps, hp - 1)
                    if half and hp == HP - 1:
                        dve.wait_ge(ao_ps, HP + 1)
                    for odd in range(2):
                        a = att[:, att_slot(i), odd, :]
                        o = bank[4 + 2 * (i % 2) + odd]
                        if half:
                            nc.vector.tensor_tensor(a.rearrange("p (u i) -> p u i", u=NU),
                                                    o[:].rearrange("p (u i) -> p u i", u=NU),
                                                    keep_both[:].rearrange("p (a s) i -> p a (s i)", a=1)
                                                    .broadcast_to([P, NU, P]), ALU.mult).then_inc(att_done, 1)
                            continue
                        for s in range(2):
                            r, c = slice(s * GQ, (s + 1) * GQ), slice(s * GQ, (s + 1) * GQ)
                            nc.vector.tensor_tensor(a[r, :].rearrange("p (u i) -> p u i", u=NU)[:, :, c],
                                                    o[r, :].rearrange("p (u i) -> p u i", u=NU)[:, :, c],
                                                    keep[r, c].rearrange("p (a i) -> p a i", a=1)
                                                    .broadcast_to([GQ, NU, GQ]), ALU.mult).then_inc(att_done, 1)

                def even_values(u):
                    dve.wait_ge(v_ps, NU + u + 1)
                    nc.vector.tensor_copy(vv_both[GQ:P, 2 * u, :], value_bank(1, u)[GQ:P, :]).then_inc(v_even_done, 1)

                if half == 0:
                    dve.wait_ge(att_zeroed, 1)
                clip(0)
                after("clip0")
                scan(0)
                after("scan0")
                clip(1)
                after("clip1")
                scaled_key_query(0)
                if half:
                    even_values(0)
                scaled_key_query(1)
                if half:
                    for u in range(1, V_DVE):
                        even_values(u)
                scan(1)
                after("scan1")
                after("first")
                for hp in range(HP):
                    mask_scores(hp)
                    if hp + 2 < HP:
                        scaled_key_query(hp + 2)
                    after(f"pair{hp}")

                tiles = slice(half * NU, (half + 1) * NU)
                h1 = rows[:, tiles, 0:D]
                dve.wait_ge(res_in, 16 * (half + 1))
                dve.wait_ge(y_ps, half + 1)
                nc.vector.tensor_tensor(h1, h1, bank[2][:].rearrange("p (u d) -> p u d", u=NU), ALU.add)\
                    .then_inc(h1_done, 1)
                dve.wait_ge(h1_done, half + 1)
                after("project")
                moments(lambda u: rows[:, half * NU + u, 0:D], stats)
                nc.vector.tensor_scalar_add(tiny[:, :, 1], mv[:, :, 1], LN_EPS).then_inc(var2_done, 1)
                dve.wait_ge(scale2_done, half + 1)

                def over_x(ap):
                    return ap.rearrange("p (u a) -> p u a", a=1).broadcast_to([P, NU, NX])

                def over_u(ap):
                    return ap.rearrange("p (a x) -> p a x", a=1).broadcast_to([P, NU, NX])

                dve.wait_ge(lg_ps, half + 1)
                if half:
                    dve.wait_ge(ex_done, half)
                link(nc.vector.tensor_tensor(lg[:], bank[3][:, 0:NU * NX].rearrange("p (u x) -> p u x", u=NU),
                                             over_x(scale[:]), ALU.mult))
                link(nc.vector.tensor_tensor(lg[:], lg[:], over_u(bs_bc[:]), ALU.add))
                link(nc.vector.tensor_reduce(mx[:], lg[:], AX.X, ALU.max))
                nc.vector.tensor_tensor(lg[:], lg[:], over_x(mx[:]), ALU.subtract).then_inc(lm_done, 1)
                dve.wait_ge(lm_done, half + 1)
                link(nc.vector.scalar_tensor_tensor(cand[:], lg[:], 0.0, over_u(rev[:]), ALU.is_ge, ALU.mult))
                link(nc.vector.tensor_reduce(cm[:, tiles], cand[:], AX.X, ALU.max))
                nc.vector.tensor_tensor(ohb[:, tiles, :], cand[:], over_x(cm[:, tiles]), ALU.is_equal).then_inc(oh_done, 1)
                link(nc.vector.tensor_copy(rows[:, tiles, D], mv[:, :, 0]))
                link(nc.vector.tensor_copy(rows[:, tiles, D + 1], scale[:]))
                dve.wait_ge(ex_done, half + 1)
                link(nc.vector.tensor_reduce(esum[:], ex[:], AX.X, ALU.add))
                link(nc.vector.reciprocal(rows[:, tiles, D + 2], esum[:]))
                after("route")

            slots(1)
            dve.wait_ge(cnt_ps, 2)
            tiles_before(first)
            link(nc.vector.tensor_tensor(last[:], first[:], ntile[:], ALU.add))
            link(nc.vector.tensor_tensor(owner_c[:], tile_no[:].rearrange("p (t a) -> p t a", a=1).broadcast_to([P, TILES, NX]),
                                         last[:].rearrange("p (a x) -> p a x", a=1).broadcast_to([P, TILES, NX]), ALU.is_ge))
            link(nc.vector.tensor_reduce(owner_r[:], owner_c[:], AX.X, ALU.add))
            link(nc.vector.tensor_scalar_min(owner_f[:], owner_r[:], float(NX - 1)))
            nc.vector.tensor_copy(owner_i[:], owner_f[:]).then_inc(owner_done, 1)
            def over_tiles(ap):
                return ap.rearrange("p (a x) -> p a x", a=1).broadcast_to([P, TILES, NX])

            link(nc.vector.tensor_tensor(shift[:], region[:], first[:], ALU.subtract))
            link(nc.vector.tensor_tensor(chosen[:], owner_f[:].rearrange("p (t a) -> p t a", a=1).broadcast_to([P, TILES, NX]),
                                         over_tiles(expert_no[:]), ALU.is_equal))
            link(nc.vector.tensor_tensor(chosen[:], chosen[:], over_tiles(shift[:]), ALU.mult))
            link(nc.vector.tensor_reduce(place[:], chosen[:], AX.X, ALU.add))
            link(nc.vector.tensor_tensor(place[:], place[:], tile_no[:], ALU.add))
            link(nc.vector.tensor_scalar(unused[:], owner_r[:], float(NX), float(REGION_TILES), ALU.is_ge, ALU.mult))
            link(nc.vector.scalar_tensor_tensor(place[:], place[:], float(REGION_TILES), unused[:], ALU.min, ALU.max))
            link(nc.vector.tensor_scalar_mul(place[:], place[:], float(P)))
            nc.vector.tensor_copy(place_i[:], place[:]).then_inc(place_done, 1)

            def normalise(j):
                dve.wait_ge(srow_in[j % 4], 16 * (j // 4 + 1))
                if j >= 4:
                    dve.wait_ge(sxT_ps, j - 3)
                nc.vector.tensor_scalar(sx[:, j % 4, :], srow[:, j, 0:D], srow[:, j, D:D + 1], srow[:, j, D + 1:D + 2],
                                        ALU.subtract, ALU.mult).then_inc(sx_done, 1)

            dve.wait_ge(owner_done, 1)

            def take_weights(j):
                if j == 0:
                    dve.wait_ge(w1_in, 32)
                    dve.wait_ge(w2_in, 16)
                if j >= 3:
                    dve.wait_ge(ffn_ps, j - 2)
                owner = dve.value_load(owner_i[0:1, j:j + 1], min_val=0, max_val=NX - 1)
                nc.vector.tensor_copy(w1_now[:, j % 3, :], flat[:, bass.ds(owner * FB, FB)]).then_inc(w_now, 1)
                nc.vector.tensor_copy(w2_now[j % 3], w2_sb[:, bass.ds(owner * F, F)]).then_inc(w_now, 1)

            def finish(j):
                dve.wait_ge(ffn_ps, j + 1)
                if j >= 4:
                    dve.wait_ge(stored[j % 4], 16 * (j // 4))
                nc.vector.scalar_tensor_tensor(fin[:, j % 4, :], bank[6 + j % 2][:, 0:D], srow[:, j, D + 2:D + 3],
                                               srow[:, j, 0:D], ALU.mult, ALU.add).then_inc(fin_done, 1)
                nc.vector.tensor_scalar_add(dest[:, j:j + 1], srow[:, j, D + 3:D + 4], NO_TOKEN).then_inc(dest_done, 1)

            take_weights(0)
            take_weights(1)
            normalise(0)
            normalise(1)
            normalise(2)
            for j in range(TILES + 1):
                if j + 3 < TILES:
                    normalise(j + 3)
                if j >= 1:
                    finish(j - 1)
                if j + 2 < TILES:
                    take_weights(j + 2)

        @block.tensor
        def _(pe):
            ahead = Ahead(PE_AHEAD)

            def multiply_chunk(n):
                half, c = divmod(n, NCH)
                v = chunk_view(n)
                for i, (t, k) in enumerate(rows_of(c)):
                    pe.wait_ge(masked, TC * n + i + 1)
                    for s in range(2):
                        mm = nc.tensor.matmul(sums(half)[s * B:(s + 1) * B, :], xT[0:k, t, :],
                                              v[0:k, s * NU:(s + 1) * NU, i, :],
                                              start=(t == GT - 1), stop=(t == GT - 2), tile_position=(0, s * B))
                mm.then_inc(used, 1)

            def keep_clock(n):
                for _ in range(n):
                    nc.tensor.matmul(bank[7][:], ones_bf[:], restart[:, 0:HTOK], start=True, stop=True)

            pe.wait_ge(x_in, 32)
            for n in range(NCH):
                if n == 5:
                    pe.wait_ge(const_pool, NCONST)
                    pe.wait_ge(small_in, 16 * 6)
                    nc.tensor.matmul(bank[3][:, 0:NX], mean_w[:], ws_sb[:], start=True, stop=True).then_inc(colmean_ps, 1)
                multiply_chunk(n)
            pe.wait_ge(bias_done, 1)
            pe.wait_ge(const_dve, 2)
            pe.wait_ge(wc_done, 1)

            def ranks(half):
                pe.wait_ge(oh_done, half + 1)
                pe.wait_ge(lm_done, half + 1)
                ohf = ohb[:].rearrange("p t x -> p (t x)")
                t0, t1 = half * NU, (half + 1) * NU
                mm = nc.tensor.matmul(bank[3][:, 0:NU * NX], earlier[:], ohf[:, t0 * NX:t1 * NX],
                                      start=True, stop=False)
                for k in range(1, t1):
                    u0 = max(0, k - t0)
                    mm = nc.tensor.matmul(bank[3][:, u0 * NX:NU * NX], ones_bf[:], ohf[:, (t0 + u0 - k) * NX:(t1 - k) * NX],
                                          start=False, stop=(k == t1 - 1))
                mm.then_inc(rank_ps, 1)
                for t in range(t1):
                    mm = nc.tensor.matmul(bank[2][:, 0:NX], ones_bf[:], ohb[:, t, :], start=(t == 0), stop=(t == t1 - 1))
                mm.then_inc(cnt_ps, 1)

            for half in range(2):
                def after(stage):
                    for n in ahead.after(stage, half):
                        multiply_chunk(n)

                after("start")
                if half:
                    ranks(0)
                    pe.wait_ge(h1T_done, half)
                    pe.wait_ge(att_done, att_count(HP))
                    keep_clock(WARM_NORM)
                for u in range(NU):
                    pe.wait_ge(xn_done, half * NU + u + 1)
                    mm = nc.tensor.transpose(bank[1][:, u * P:(u + 1) * P], xn[:, u, :], ident[:])
                mm.then_inc(xnT_ps, 1)
                if half:
                    keep_clock(WARM_GATES)
                after("norm")
                pe.wait_ge(xnT_done, half + 1)
                pe.wait_ge(wa_in, 16)
                def gates(g):
                    for hp in (2 * g, 2 * g + 1):
                        nc.tensor.matmul(bank[4 + hp][:], wa_sb[:, hp * P:(hp + 1) * P], xnT[:], start=True, stop=True)\
                            .then_inc(gate_ps, 1)

                def values(u):
                    if u < 2:
                        pe.wait_ge(k_raw if u == 0 else q_raw, half * HP + 2)
                    elif half == 0:
                        pe.wait_ge(v_done, u - 1)
                    o = value_bank(half, u)
                    if half == 0:
                        nc.tensor.matmul(o[:], xnT[:, u * P:(u + 1) * P], wqkv_sb[:, 2 * INNER:3 * INNER],
                                         start=True, stop=False)
                        mm = nc.tensor.matmul(o[:], sel0[:], bias_b[:, BV], start=False, stop=True)
                    else:
                        for s in range(2):
                            c = (1 - s) * GQ
                            nc.tensor.matmul(o[c:c + GQ, :], xnT[:, u * P + s * GQ:u * P + (s + 1) * GQ],
                                             wqkv_sb[:, 2 * INNER:3 * INNER], start=True, stop=False, tile_position=(0, c))
                        for s in range(2):
                            c = (1 - s) * GQ
                            mm = nc.tensor.matmul(o[c:c + GQ, :], sel0[:, 0:GQ], bias_b[:, BV], start=False, stop=True,
                                                  tile_position=(0, c))
                    mm.then_inc(v_ps, 1)

                def all_values_done():
                    pe.wait_ge(v_done, NU if half == 0 else NU + 2 * NU - V_DVE)
                    if half:
                        pe.wait_ge(v_even_done, V_DVE)

                def keys_queries(hp):
                    i = half * HP + hp
                    if hp == 2:
                        all_values_done()
                    if hp:
                        pe.wait_ge(k_raw, i)
                    elif half:
                        pe.wait_ge(slot_done, half)
                    nc.tensor.matmul(bank[2][:], wqkv_sb[:, INNER + hp * P:INNER + (hp + 1) * P], xnT[:],
                                     start=True, stop=True).then_inc(k_ps, 1)
                    if hp:
                        pe.wait_ge(q_raw, i)
                    elif half:
                        pe.wait_ge(slot_done, half)
                    nc.tensor.matmul(bank[3][:], wqkv_sb[:, hp * P:(hp + 1) * P], xnT[:],
                                     start=True, stop=True).then_inc(q_ps, 1)

                def scores(hp):
                    i = half * HP + hp
                    pe.wait_ge(k_done, i + 1)
                    pe.wait_ge(q_done, i + 1)
                    pe.wait_ge(gate_exp, HP * (half + 1))
                    if i >= 2:
                        pe.wait_ge(att_done, att_count(i - 1))
                    for u in range(NU):
                        for odd in range(2):
                            r = slice(odd * DH, (odd + 1) * DH)
                            o = bank[4 + 2 * (i % 2) + odd]
                            for s in range(2):
                                t = slice(u * P + s * GQ, u * P + (s + 1) * GQ)
                                for key_half in range(half + 1):
                                    c = (s ^ key_half) * GQ
                                    mm = nc.tensor.matmul(o[c:c + GQ, t], ks[r, key_half, hp, t], qs[r, i % 2, t],
                                                          start=True, stop=True, tile_position=(odd * DH, c))
                    mm.then_inc(sim_ps, 1)

                def mix(hp):
                    i = half * HP + hp
                    if hp == 0:
                        pe.wait_ge(xnT_done, half + 1)
                        all_values_done()
                        if half:
                            pe.wait_ge(vv_moved, 32)
                    else:
                        pe.wait_ge(ao_done, i)
                    pe.wait_ge(att_done, att_count(i + 1))
                    w = GQ if half else P
                    for g in range(HTOK // w):
                        t = slice(g * w, (g + 1) * w)
                        for odd in range(2):
                            h = 2 * hp + odd
                            v = (vv_both if half else vv)[:, g, h * DH:(h + 1) * DH]
                            mm = nc.tensor.matmul(bank[1][odd * DH:(odd + 1) * DH, t], v, att[:, att_slot(i), odd, t],
                                                  start=True, stop=True, tile_position=(0, odd * DH))
                    mm.then_inc(ao_ps, 1)

                def project(hps):
                    if hps[0] == 0:
                        pe.wait_ge(k_raw, HP * (half + 1))
                        nc.tensor.matmul(bank[2][:].rearrange("p (u d) -> p u d", u=NU), sel0[:],
                                         bias_b[:, BO].rearrange("p (a d) -> p a d", a=1).broadcast_to([3 * NX, NU, D]),
                                         start=True, stop=False)
                    for hp in hps:
                        pe.wait_ge(ao_done, HP * half + hp + 1)
                        for u in range(NU):
                            mm = nc.tensor.matmul(bank[2][:, u * P:(u + 1) * P], aoT[:, hp, u * P:(u + 1) * P],
                                                  wout_sb[:, hp, :], start=False, stop=(u == NU - 1 and hp == HP - 1))
                    return mm

                gates(0)
                pe.wait_ge(wqk_in, 16)
                keys_queries(0)
                gates(1)
                keys_queries(1)
                after("gates")
                pe.wait_ge(wv_in, 16)
                for u in range(NU):
                    values(u)
                after("values")
                scores(0)
                after("first")
                for hp in range(HP):
                    if hp + 2 < HP:
                        keys_queries(hp + 2)
                    if hp + 1 < HP:
                        scores(hp + 1)
                    else:
                        pe.wait_ge(wout_in, 16)
                        project(range(HP - 1))
                    mix(hp)
                    after(f"pair{hp}")
                project([HP - 1]).then_inc(y_ps, 1)
                after("project")
                pe.wait_ge(h1_done, half + 1)
                for u in range(NU):
                    mm = nc.tensor.transpose(bank[1][:, u * P:(u + 1) * P], rows[:, half * NU + u, 0:D], ident[:])
                mm.then_inc(h1T_ps, 1)
                pe.wait_ge(h1T_done, half + 1)
                pe.wait_ge(q_raw, HP * (half + 1))
                for u in range(NU):
                    mm = nc.tensor.matmul(bank[3][:, u * NX:(u + 1) * NX], h1T[:, u * P:(u + 1) * P], wc_sb[:],
                                          start=True, stop=True)
                mm.then_inc(lg_ps, 1)
                after("route")

            ranks(1)

            keep_clock(WARM_FFN)

            def transpose_rows(j):
                pe.wait_ge(sx_done, j + 1)
                if j >= 2:
                    pe.wait_ge(sxT_done, j - 1)
                nc.tensor.transpose(bank[j % 2][:, 0:P], sx[:, j % 4, :], ident[:]).then_inc(sxT_ps, 1)

            def expand(j):
                pe.wait_ge(sxT_done, j + 1)
                pe.wait_ge(w_now, 2 * j + 2)
                if j >= 2:
                    pe.wait_ge(hid_done, FC * (j - 1))
                w1v = w1_now[:, j % 3, 0:F].rearrange("p (f c) -> p c f", c=FC)
                for c in range(FC):
                    mm = nc.tensor.matmul(bank[2 + j % 2][:, c * P:(c + 1) * P], w1v[:, c, :], sxT[:, j % 4, :],
                                          start=True, stop=True)
                mm.then_inc(hid_ps, 1)

            def contract(j):
                pe.wait_ge(hid_done, FC * (j + 1))
                if j >= 2:
                    pe.wait_ge(fin_done, j - 1)
                if j == 0:
                    pe.wait_ge(pick_done, 1)
                o = bank[6 + j % 2][:, 0:D]
                nc.tensor.matmul(o, pick[:, j, :], bias_b[:, B2], start=True, stop=False)
                for c in range(FC):
                    mm = nc.tensor.matmul(o, hid[:, j % 2, c * P:(c + 1) * P], w2_now[j % 3][:, c * D:(c + 1) * D],
                                          start=False, stop=(c == FC - 1))
                mm.then_inc(ffn_ps, 1)

            transpose_rows(0)
            for j in range(TILES + 1):
                if j < TILES:
                    expand(j)
                if j == 0:
                    transpose_rows(1)
                if j >= 1:
                    contract(j - 1)
                if j + 2 < TILES:
                    transpose_rows(j + 2)


def kernel(x, L0_tok_weight, L0_tok_bias, L0_tok_mask, L0_attn_gamma, L0_attn_w_qkv, L0_attn_b_qkv, L0_attn_w_a,
           L0_attn_b_a, L0_attn_w_out, L0_attn_b_out, L0_ffn_Ws, L0_ffn_bs, L0_ffn_W1, L0_ffn_b1, L0_ffn_W2,
           L0_ffn_b2):
    import numpy as np
    import concourse.bacc as bacc
    from concourse.bass_utils import run_bass_kernel_spmd

    def by_partition(v):
        return np.ascontiguousarray(np.asarray(v).reshape(-1, P).T)

    bqkv = np.asarray(L0_attn_b_qkv)
    arrays = {
        "x_t": np.ascontiguousarray(np.asarray(x).T),
        "weight": np.asarray(L0_tok_weight),
        "tok_bias": np.asarray(L0_tok_bias),
        "mask": np.asarray(L0_tok_mask),
        "gamma": by_partition(L0_attn_gamma),
        "w_qkv": np.asarray(L0_attn_w_qkv),
        "bq": by_partition(bqkv[0:INNER]),
        "bk": by_partition(bqkv[INNER:2 * INNER]),
        "b_v": bqkv[2 * INNER:3 * INNER].reshape(1, INNER),
        "w_a": np.asarray(L0_attn_w_a),
        "ba": by_partition(L0_attn_b_a),
        "w_out": np.asarray(L0_attn_w_out),
        "b_out": np.asarray(L0_attn_b_out).reshape(1, D),
        "w_s": np.asarray(L0_ffn_Ws),
        "b_s": np.asarray(L0_ffn_bs).reshape(1, NX),
        "w1": np.asarray(L0_ffn_W1),
        "b1": np.asarray(L0_ffn_b1),
        "w2": np.asarray(L0_ffn_W2),
        "b2": np.asarray(L0_ffn_b2),
    }
    nc = bacc.Bacc("TRN2", target_bir_lowering=False, num_devices=1)
    feeds, aps = {}, {}
    for name, a in arrays.items():
        feeds[f"in_{name}"] = np.ascontiguousarray(a)
        aps[name] = nc.dram_tensor(f"in_{name}", a.shape, mybir.dt.from_np(a.dtype), kind="ExternalInput").ap()
    aps["out"] = nc.dram_tensor("out_tower", (B, E, D), F32, kind="ExternalOutput").ap()
    build(nc, **aps)
    r = run_bass_kernel_spmd(nc, [feeds], core_ids=[0])
    return r.results[0]["out_tower"]
```
